# Optimizing a Trainium2 kernel written in Bass

```python
import numpy as np
import jax
import jax.numpy as jnp

def _softmax(x, axis=-1):
    return jax.nn.softmax(x, axis=axis)

def _gelu(x):
    return jax.nn.gelu(x, approximate=True)

def _silu(x):
    return jax.nn.silu(x)

def _sigmoid(x):
    return jax.nn.sigmoid(x)

def _layernorm(x, axis=-1, eps=1e-05):
    m = jnp.mean(x, axis=axis, keepdims=True)
    v = jnp.var(x, axis=axis, keepdims=True)
    return (x - m) / jnp.sqrt(v + eps)

def _scatter_add(tgt, idx, src, axis=0):
    return tgt.at[idx].add(src)

def _segment_sum(src, seg, n):
    return jax.ops.segment_sum(src, seg, n)
kernel_name = 'mk_conv_seq_d4_conv_nchw512_r2_ba6bea'

def setup_inputs(seed: int=0):
    np.random.seed(seed)
    _w = jnp.asarray

    def _rec_inputs():
        import jax
        import jax.numpy as jnp
        _gk = jax.random.key(seed)
        x = -0.0002928 + 1 * jax.random.normal(jax.random.fold_in(_gk, 1), (8, 256, 32, 32), jnp.float32)
        return x
    x = _rec_inputs()

    def _L0_conv_setup():
        import jax, jax.numpy as jnp
        import numpy as np
        CH = 256
        HEADS = 8
        GROUPS = 32
        EPS = 1e-05

        def _group_norm(x, w, b):
            B, C, T = x.shape
            xg = x.reshape(B, GROUPS, C // GROUPS * T)
            mean = xg.mean(axis=2, keepdims=True)
            var = xg.var(axis=2, keepdims=True)
            xg = (xg - mean) * jax.lax.rsqrt(var + EPS)
            xn = xg.reshape(B, C, T)
            return xn * w[None, :, None] + b[None, :, None]
        key = jax.random.key(seed)
        ks = jax.random.split(key, 7)
        b, c, h, w = (8, CH, 32, 32)
        x = jax.random.normal(ks[0], (b, c, h, w), dtype=jnp.float32)
        gn_w = jax.random.normal(ks[1], (c,), dtype=jnp.float32) * 0.1 + 1.0
        gn_b = jax.random.normal(ks[2], (c,), dtype=jnp.float32) * 0.1
        qkv_w = jax.random.normal(ks[3], (3 * c, c), dtype=jnp.float32) / np.sqrt(c)
        qkv_b = jax.random.normal(ks[4], (3 * c,), dtype=jnp.float32) * 0.02
        proj_w = jax.random.normal(ks[5], (c, c), dtype=jnp.float32) / np.sqrt(c)
        proj_b = jax.random.normal(ks[6], (c,), dtype=jnp.float32) * 0.02
        return {'x': x, 'gn_w': gn_w, 'gn_b': gn_b, 'qkv_w': qkv_w, 'qkv_b': qkv_b, 'proj_w': proj_w, 'proj_b': proj_b}
    _L0_conv_all = _L0_conv_setup()
    _L0_conv_in = {k: v for k, v in _L0_conv_all.items() if k in ('gn_w', 'gn_b', 'qkv_w', 'qkv_b', 'proj_w', 'proj_b')}
    del _L0_conv_all

    def _L1_conv_setup():
        import jax, jax.numpy as jnp
        import numpy as np
        import math
        B, C, H, W = (8, 256, 32, 32)
        NH = 8
        G = 32
        EPS = 1e-06

        def group_norm(x, gamma, beta, groups=G, eps=EPS):
            b, c, h, w = x.shape
            xr = x.reshape(b, groups, c // groups, h, w)
            mu = xr.mean(axis=(2, 3, 4), keepdims=True)
            var = xr.var(axis=(2, 3, 4), keepdims=True)
            xn = ((xr - mu) * jax.lax.rsqrt(var + eps)).reshape(b, c, h, w)
            return xn * gamma[None, :, None, None] + beta[None, :, None, None]

        def conv2d(x, w, b, pad):
            y = jax.lax.conv_general_dilated(x, w, window_strides=(1, 1), padding=[(pad, pad), (pad, pad)], dimension_numbers=('NCHW', 'OIHW', 'NCHW'))
            return y + b[None, :, None, None]
        key = jax.random.key(seed)
        ks = jax.random.split(key, 20)

        def n(k, shape, s=0.02):
            return jax.random.normal(k, shape, dtype=jnp.float32) * s
        f32 = jnp.float32
        return {'hidden_states': jax.random.normal(ks[0], (B, C, H, W), dtype=f32), 'pre_g': jnp.ones(C, f32), 'pre_b': jnp.zeros(C, f32), 'norm_g': jnp.ones(C, f32), 'norm_b': jnp.zeros(C, f32), 'post_g': jnp.ones(C, f32), 'post_b': jnp.zeros(C, f32), 'pos_emb': n(ks[1], (1, C, 32, 32)), 'wq': n(ks[2], (C, C)), 'wk': n(ks[3], (C, C)), 'wv': n(ks[4], (C, C)), 'wq0': n(ks[5], (C // 2, C)), 'wq1': n(ks[6], (C // 2, C)), 'wk0': n(ks[7], (C // 2, C)), 'wk1': n(ks[8], (C // 2, C)), 'wv0': n(ks[9], (C // 2, C)), 'wv1': n(ks[10], (C // 2, C)), 'sa_w1': n(ks[11], (C // 8, C, 1, 1)), 'sa_b1': jnp.zeros(C // 8, f32), 'sa_w2': n(ks[12], (C // 8, C // 8, 3, 3)), 'sa_b2': jnp.zeros(C // 8, f32), 'sa_w3': n(ks[13], (1, C // 8, 1, 1)), 'sa_b3': jnp.zeros(1, f32), 'ff_w1': n(ks[14], (C, 2 * C)), 'ff_b1': jnp.zeros(C, f32), 'ff_w2': n(ks[15], (C, C)), 'ff_b2': jnp.zeros(C, f32), 'out_w': n(ks[16], (C, C)), 'out_b': jnp.zeros(C, f32)}
    _L1_conv_all = _L1_conv_setup()
    _L1_conv_in = {k: v for k, v in _L1_conv_all.items() if k in ('pre_g', 'pre_b', 'norm_g', 'norm_b', 'post_g', 'post_b', 'pos_emb', 'wq', 'wk', 'wv', 'wq0', 'wq1', 'wk0', 'wk1', 'wv0', 'wv1', 'sa_w1', 'sa_b1', 'sa_w2', 'sa_b2', 'sa_w3', 'sa_b3', 'ff_w1', 'ff_b1', 'ff_w2', 'ff_b2', 'out_w', 'out_b')}
    del _L1_conv_all

    def _L2_conv_setup():
        import jax, jax.numpy as jnp
        import numpy as np
        import math
        C = 256
        N_HEADS = 8
        N_GROUPS = 32
        EPS = 1e-05
        key = jax.random.key(seed)
        k1, k2, k3 = jax.random.split(key, 3)
        B, H, W = (4, 48, 48)
        x = jax.random.normal(k1, (B, C, H, W), dtype=jnp.float32)
        gn_w = jnp.ones((C,), jnp.float32)
        gn_b = jnp.zeros((C,), jnp.float32)
        qkv_w = jax.random.normal(k2, (3 * C, C), jnp.float32) * (1.0 / math.sqrt(C))
        qkv_b = jnp.zeros((3 * C,), jnp.float32)
        proj_w = jax.random.normal(k3, (C, C), jnp.float32) * (1.0 / math.sqrt(C))
        proj_b = jnp.zeros((C,), jnp.float32)
        return {'x': x, 'gn_w': gn_w, 'gn_b': gn_b, 'qkv_w': qkv_w, 'qkv_b': qkv_b, 'proj_w': proj_w, 'proj_b': proj_b}
    _L2_conv_all = _L2_conv_setup()
    _L2_conv_in = {k: v for k, v in _L2_conv_all.items() if k in ('gn_w', 'gn_b', 'qkv_w', 'qkv_b', 'proj_w', 'proj_b')}
    del _L2_conv_all

    def _L3_conv_setup():
        import jax, jax.numpy as jnp
        import numpy as np
        import math
        B, C, H, W = (16, 256, 32, 32)
        GROUPS = 32
        EPS = 1e-05

        def group_norm(x, w, b):
            Bx, Cx, Hx, Wx = x.shape
            xg = x.reshape(Bx, GROUPS, Cx // GROUPS, Hx, Wx)
            mean = xg.mean(axis=(2, 3, 4), keepdims=True)
            var = xg.var(axis=(2, 3, 4), keepdims=True)
            xg = (xg - mean) * jax.lax.rsqrt(var + EPS)
            xn = xg.reshape(Bx, Cx, Hx, Wx)
            return xn * w[None, :, None, None] + b[None, :, None, None]
        key = jax.random.key(seed)
        ks = jax.random.split(key, 4)
        x = jax.random.normal(ks[0], (B, C, H, W), dtype=jnp.float32)
        gn_w = jnp.ones((C,), dtype=jnp.float32)
        gn_b = jnp.zeros((C,), dtype=jnp.float32)
        qkv_w = jax.random.normal(ks[1], (3 * C, C), dtype=jnp.float32) * (1.0 / math.sqrt(C))
        qkv_b = jnp.zeros((3 * C,), dtype=jnp.float32)
        out_w = jax.random.normal(ks[2], (C, C), dtype=jnp.float32) * (1.0 / math.sqrt(C))
        out_b = jnp.zeros((C,), dtype=jnp.float32)
        return {'x': x, 'gn_w': gn_w, 'gn_b': gn_b, 'qkv_w': qkv_w, 'qkv_b': qkv_b, 'out_w': out_w, 'out_b': out_b}
    _L3_conv_all = _L3_conv_setup()
    _L3_conv_in = {k: v for k, v in _L3_conv_all.items() if k in ('gn_w', 'gn_b', 'qkv_w', 'qkv_b', 'out_w', 'out_b')}
    del _L3_conv_all
    return {'x': x, 'L0_conv_gn_w': _L0_conv_in['gn_w'], 'L0_conv_gn_b': _L0_conv_in['gn_b'], 'L0_conv_qkv_w': _L0_conv_in['qkv_w'], 'L0_conv_qkv_b': _L0_conv_in['qkv_b'], 'L0_conv_proj_w': _L0_conv_in['proj_w'], 'L0_conv_proj_b': _L0_conv_in['proj_b'], 'L1_conv_pre_g': _L1_conv_in['pre_g'], 'L1_conv_pre_b': _L1_conv_in['pre_b'], 'L1_conv_norm_g': _L1_conv_in['norm_g'], 'L1_conv_norm_b': _L1_conv_in['norm_b'], 'L1_conv_post_g': _L1_conv_in['post_g'], 'L1_conv_post_b': _L1_conv_in['post_b'], 'L1_conv_pos_emb': _L1_conv_in['pos_emb'], 'L1_conv_wq': _L1_conv_in['wq'], 'L1_conv_wk': _L1_conv_in['wk'], 'L1_conv_wv': _L1_conv_in['wv'], 'L1_conv_wq0': _L1_conv_in['wq0'], 'L1_conv_wq1': _L1_conv_in['wq1'], 'L1_conv_wk0': _L1_conv_in['wk0'], 'L1_conv_wk1': _L1_conv_in['wk1'], 'L1_conv_wv0': _L1_conv_in['wv0'], 'L1_conv_wv1': _L1_conv_in['wv1'], 'L1_conv_sa_w1': _L1_conv_in['sa_w1'], 'L1_conv_sa_b1': _L1_conv_in['sa_b1'], 'L1_conv_sa_w2': _L1_conv_in['sa_w2'], 'L1_conv_sa_b2': _L1_conv_in['sa_b2'], 'L1_conv_sa_w3': _L1_conv_in['sa_w3'], 'L1_conv_sa_b3': _L1_conv_in['sa_b3'], 'L1_conv_ff_w1': _L1_conv_in['ff_w1'], 'L1_conv_ff_b1': _L1_conv_in['ff_b1'], 'L1_conv_ff_w2': _L1_conv_in['ff_w2'], 'L1_conv_ff_b2': _L1_conv_in['ff_b2'], 'L1_conv_out_w': _L1_conv_in['out_w'], 'L1_conv_out_b': _L1_conv_in['out_b'], 'L2_conv_gn_w': _L2_conv_in['gn_w'], 'L2_conv_gn_b': _L2_conv_in['gn_b'], 'L2_conv_qkv_w': _L2_conv_in['qkv_w'], 'L2_conv_qkv_b': _L2_conv_in['qkv_b'], 'L2_conv_proj_w': _L2_conv_in['proj_w'], 'L2_conv_proj_b': _L2_conv_in['proj_b'], 'L3_conv_gn_w': _L3_conv_in['gn_w'], 'L3_conv_gn_b': _L3_conv_in['gn_b'], 'L3_conv_qkv_w': _L3_conv_in['qkv_w'], 'L3_conv_qkv_b': _L3_conv_in['qkv_b'], 'L3_conv_out_w': _L3_conv_in['out_w'], 'L3_conv_out_b': _L3_conv_in['out_b']}

def reference(x, L0_conv_gn_w, L0_conv_gn_b, L0_conv_qkv_w, L0_conv_qkv_b, L0_conv_proj_w, L0_conv_proj_b, L1_conv_pre_g, L1_conv_pre_b, L1_conv_norm_g, L1_conv_norm_b, L1_conv_post_g, L1_conv_post_b, L1_conv_pos_emb, L1_conv_wq, L1_conv_wk, L1_conv_wv, L1_conv_wq0, L1_conv_wq1, L1_conv_wk0, L1_conv_wk1, L1_conv_wv0, L1_conv_wv1, L1_conv_sa_w1, L1_conv_sa_b1, L1_conv_sa_w2, L1_conv_sa_b2, L1_conv_sa_w3, L1_conv_sa_b3, L1_conv_ff_w1, L1_conv_ff_b1, L1_conv_ff_w2, L1_conv_ff_b2, L1_conv_out_w, L1_conv_out_b, L2_conv_gn_w, L2_conv_gn_b, L2_conv_qkv_w, L2_conv_qkv_b, L2_conv_proj_w, L2_conv_proj_b, L3_conv_gn_w, L3_conv_gn_b, L3_conv_qkv_w, L3_conv_qkv_b, L3_conv_out_w, L3_conv_out_b):
    import jax
    import jax.numpy as jnp

    def _L0_conv_ref(x, gn_w, gn_b, qkv_w, qkv_b, proj_w, proj_b):
        import jax, jax.numpy as jnp
        import numpy as np
        CH = 256
        HEADS = 8
        GROUPS = 32
        EPS = 1e-05

        def _group_norm(x, w, b):
            B, C, T = x.shape
            xg = x.reshape(B, GROUPS, C // GROUPS * T)
            mean = xg.mean(axis=2, keepdims=True)
            var = xg.var(axis=2, keepdims=True)
            xg = (xg - mean) * jax.lax.rsqrt(var + EPS)
            xn = xg.reshape(B, C, T)
            return xn * w[None, :, None] + b[None, :, None]
        b, c, *spatial = x.shape
        T = int(np.prod(spatial))
        xf = x.reshape(b, c, T)
        xn = _group_norm(xf, gn_w, gn_b)
        qkv = jnp.einsum('oc,bct->bot', qkv_w, xn) + qkv_b[None, :, None]
        qkv = qkv.reshape(b * HEADS, 3 * c // HEADS, T)
        ch = qkv.shape[1] // 3
        q, k, v = jnp.split(qkv, 3, axis=1)
        scale = 1.0 / np.sqrt(np.sqrt(ch))
        weight = jnp.einsum('bct,bcs->bts', q * scale, k * scale)
        weight = jax.nn.softmax(weight.astype(jnp.float32), axis=-1).astype(weight.dtype)
        h = jnp.einsum('bts,bcs->bct', weight, v)
        h = h.reshape(b, c, T)
        h = jnp.einsum('oc,bct->bot', proj_w, h) + proj_b[None, :, None]
        return (xf + h).reshape(b, c, *spatial)

    def _L1_conv_ref(hidden_states, pre_g, pre_b, norm_g, norm_b, post_g, post_b, pos_emb, wq, wk, wv, wq0, wq1, wk0, wk1, wv0, wv1, sa_w1, sa_b1, sa_w2, sa_b2, sa_w3, sa_b3, ff_w1, ff_b1, ff_w2, ff_b2, out_w, out_b):
        import jax, jax.numpy as jnp
        import numpy as np
        import math
        B, C, H, W = (8, 256, 32, 32)
        NH = 8
        G = 32
        EPS = 1e-06

        def group_norm(x, gamma, beta, groups=G, eps=EPS):
            b, c, h, w = x.shape
            xr = x.reshape(b, groups, c // groups, h, w)
            mu = xr.mean(axis=(2, 3, 4), keepdims=True)
            var = xr.var(axis=(2, 3, 4), keepdims=True)
            xn = ((xr - mu) * jax.lax.rsqrt(var + eps)).reshape(b, c, h, w)
            return xn * gamma[None, :, None, None] + beta[None, :, None, None]

        def conv2d(x, w, b, pad):
            y = jax.lax.conv_general_dilated(x, w, window_strides=(1, 1), padding=[(pad, pad), (pad, pad)], dimension_numbers=('NCHW', 'OIHW', 'NCHW'))
            return y + b[None, :, None, None]
        b, c, h, w = hidden_states.shape
        S = h * w
        residual = hidden_states
        x = group_norm(hidden_states, pre_g, pre_b)
        x = x + pos_emb
        s1 = jax.nn.silu(conv2d(x, sa_w1, sa_b1, 0))
        s2 = jax.nn.silu(conv2d(s1, sa_w2, sa_b2, 1))
        spatial_weights = jax.nn.sigmoid(conv2d(s2, sa_w3, sa_b3, 0))
        spatial_enhanced = x * spatial_weights
        sh = group_norm(x, norm_g, norm_b).reshape(b, c, S).transpose(0, 2, 1)
        enc = sh
        hd = c // NH

        def split_heads(t):
            return t.reshape(b, S, NH, hd).transpose(0, 2, 1, 3)
        qh = split_heads(sh @ wq.T)
        kh = split_heads(enc @ wk.T)
        vh = split_heads(enc @ wv.T)
        scores = jnp.einsum('bhqd,bhkd->bhqk', qh, kh) / math.sqrt(hd)
        probs = jax.nn.softmax(scores, axis=-1)
        standard_out = jnp.einsum('bhqk,bhkd->bhqd', probs, vh)
        standard_out = standard_out.transpose(0, 2, 1, 3).reshape(b, S, c)
        msh = spatial_enhanced.reshape(b, c, S).transpose(0, 2, 1)
        parts = []
        for wqm, wkm, wvm in ((wq0, wk0, wv0), (wq1, wk1, wv1)):
            qm = msh @ wqm.T
            km = enc @ wkm.T
            vm = enc @ wvm.T
            sc = jnp.einsum('bqd,bkd->bqk', qm, km) / math.sqrt(qm.shape[-1])
            parts.append(jnp.einsum('bqk,bkd->bqd', jax.nn.softmax(sc, axis=-1), vm))
        multi_out = jnp.concatenate(parts, axis=-1)
        combined = jnp.concatenate([standard_out, multi_out], axis=-1)
        fused = jax.nn.silu(combined @ ff_w1.T + ff_b1) @ ff_w2.T + ff_b2
        final = fused @ out_w.T + out_b
        final = final.transpose(0, 2, 1).reshape(b, c, h, w)
        final = group_norm(final, post_g, post_b)
        return final + residual

    def _L2_conv_ref(x, gn_w, gn_b, qkv_w, qkv_b, proj_w, proj_b):
        import jax, jax.numpy as jnp
        import numpy as np
        import math
        C = 256
        N_HEADS = 8
        N_GROUPS = 32
        EPS = 1e-05
        b, c, h, w = x.shape
        T = h * w
        xf = x.reshape(b, c, T)
        xg = xf.reshape(b, N_GROUPS, c // N_GROUPS, T)
        mean = xg.mean(axis=(2, 3), keepdims=True)
        var = xg.var(axis=(2, 3), keepdims=True)
        xn = (xg - mean) * jax.lax.rsqrt(var + EPS)
        xn = xn.reshape(b, c, T) * gn_w[None, :, None] + gn_b[None, :, None]
        qkv = jnp.einsum('oc,bct->bot', qkv_w, xn) + qkv_b[None, :, None]
        ch = c // N_HEADS
        qkv = qkv.reshape(b * N_HEADS, 3 * ch, T)
        q, k, v = jnp.split(qkv, 3, axis=1)
        scale = 1.0 / math.sqrt(math.sqrt(ch))
        weight = jnp.einsum('bct,bcs->bts', q * scale, k * scale)
        weight = jax.nn.softmax(weight.astype(jnp.float32), axis=-1).astype(qkv.dtype)
        a = jnp.einsum('bts,bcs->bct', weight, v).reshape(b, c, T)
        hout = jnp.einsum('oc,bct->bot', proj_w, a) + proj_b[None, :, None]
        return (xn + hout).reshape(b, c, h, w)

    def _L3_conv_ref(x, gn_w, gn_b, qkv_w, qkv_b, out_w, out_b):
        import jax, jax.numpy as jnp
        import numpy as np
        import math
        B, C, H, W = (16, 256, 32, 32)
        GROUPS = 32
        EPS = 1e-05

        def group_norm(x, w, b):
            Bx, Cx, Hx, Wx = x.shape
            xg = x.reshape(Bx, GROUPS, Cx // GROUPS, Hx, Wx)
            mean = xg.mean(axis=(2, 3, 4), keepdims=True)
            var = xg.var(axis=(2, 3, 4), keepdims=True)
            xg = (xg - mean) * jax.lax.rsqrt(var + EPS)
            xn = xg.reshape(Bx, Cx, Hx, Wx)
            return xn * w[None, :, None, None] + b[None, :, None, None]
        Bx, Cx, Hx, Wx = x.shape
        N = Hx * Wx
        h = group_norm(x, gn_w, gn_b)
        hf = h.reshape(Bx, Cx, N)
        qkv = jnp.einsum('oc,bcn->bon', qkv_w, hf) + qkv_b[None, :, None]
        q, k, v = jnp.split(qkv, 3, axis=1)
        q = q.transpose(0, 2, 1)
        v = v.transpose(0, 2, 1)
        scale = 1.0 / math.sqrt(Cx)
        attn = jnp.einsum('bnc,bcm->bnm', q, k) * scale
        attn = jax.nn.softmax(attn, axis=-1)
        o = jnp.einsum('bnm,bmc->bnc', attn, v)
        o = o.transpose(0, 2, 1)
        o = jnp.einsum('oc,bcn->bon', out_w, o) + out_b[None, :, None]
        return x + o.reshape(Bx, Cx, Hx, Wx)

    def _gn(v, G=32, eps=1e-05):
        B_, C_, H_, W_ = v.shape
        g = v.reshape(B_, G, C_ // G, H_, W_)
        m = jnp.mean(g, axis=(2, 3, 4), keepdims=True)
        s = jnp.var(g, axis=(2, 3, 4), keepdims=True)
        return ((g - m) / jnp.sqrt(s + eps)).reshape(v.shape)

    def _ln_c(v, eps=1e-06):
        m = jnp.mean(v, axis=1, keepdims=True)
        s = jnp.var(v, axis=1, keepdims=True)
        return (v - m) / jnp.sqrt(s + eps)

    def _ln_t(v, eps=1e-05):
        m = jnp.mean(v, axis=-1, keepdims=True)
        s = jnp.var(v, axis=-1, keepdims=True)
        return (v - m) / jnp.sqrt(s + eps)

    def _to_tokens(v):
        B_, C_, H_, W_ = v.shape
        return v.reshape(B_, C_, H_ * W_).transpose(0, 2, 1)

    def _from_tokens(t, like):
        B_, C_, H_, W_ = like.shape
        return t.transpose(0, 2, 1).reshape(B_, C_, H_, W_)
    x = _L0_conv_ref(x, L0_conv_gn_w, L0_conv_gn_b, L0_conv_qkv_w, L0_conv_qkv_b, L0_conv_proj_w, L0_conv_proj_b)
    x = _L1_conv_ref(x, L1_conv_pre_g, L1_conv_pre_b, L1_conv_norm_g, L1_conv_norm_b, L1_conv_post_g, L1_conv_post_b, L1_conv_pos_emb, L1_conv_wq, L1_conv_wk, L1_conv_wv, L1_conv_wq0, L1_conv_wq1, L1_conv_wk0, L1_conv_wk1, L1_conv_wv0, L1_conv_wv1, L1_conv_sa_w1, L1_conv_sa_b1, L1_conv_sa_w2, L1_conv_sa_b2, L1_conv_sa_w3, L1_conv_sa_b3, L1_conv_ff_w1, L1_conv_ff_b1, L1_conv_ff_w2, L1_conv_ff_b2, L1_conv_out_w, L1_conv_out_b)
    x = _L2_conv_ref(x, L2_conv_gn_w, L2_conv_gn_b, L2_conv_qkv_w, L2_conv_qkv_b, L2_conv_proj_w, L2_conv_proj_b)
    x = _L3_conv_ref(x, L3_conv_gn_w, L3_conv_gn_b, L3_conv_qkv_w, L3_conv_qkv_b, L3_conv_out_w, L3_conv_out_b)
    return x

_drawn_inputs = setup_inputs


def setup_inputs(seed=0):
    import zlib

    import numpy as np

    out = dict(_drawn_inputs(seed))
    spreads = {'L1_conv_pre_g': (1.0, 0.6),
     'L1_conv_pre_b': (0.0, 0.8),
     'L1_conv_norm_g': (1.0, 0.6),
     'L1_conv_norm_b': (0.0, 0.8),
     'L1_conv_post_g': (1.0, 0.2),
     'L1_conv_post_b': (0.0, 0.28),
     'L1_conv_sa_b1': (0.0, 2.0),
     'L1_conv_sa_b2': (0.0, 2.0),
     'L1_conv_ff_b1': (0.0, 2.0),
     'L1_conv_ff_b2': (0.0, 0.663),
     'L1_conv_out_b': (0.0, 0.1),
     'L2_conv_gn_w': (1.0, 0.2),
     'L2_conv_gn_b': (0.0, 0.1),
     'L2_conv_qkv_b': (0.0, 0.1),
     'L2_conv_proj_b': (0.0, 0.1),
     'L3_conv_gn_w': (1.0, 0.2),
     'L3_conv_gn_b': (0.0, 0.1),
     'L3_conv_qkv_b': (0.0, 0.1),
     'L3_conv_out_b': (0.0, 0.1)}
    factors = {'L0_conv_gn_w': 7.044,
     'L0_conv_qkv_b': 3.905,
     'L0_conv_proj_b': 10.536,
     'L1_conv_pos_emb': 8.0,
     'L1_conv_wq': 8.0,
     'L1_conv_wk': 8.0,
     'L1_conv_wv': 7.483,
     'L1_conv_wq0': 8.0,
     'L1_conv_wq1': 8.0,
     'L1_conv_wk0': 8.0,
     'L1_conv_wk1': 8.0,
     'L1_conv_wv0': 8.0,
     'L1_conv_wv1': 8.0,
     'L1_conv_sa_w1': 8.0,
     'L1_conv_sa_w2': 8.0,
     'L1_conv_sa_w3': 8.0,
     'L1_conv_ff_w1': 5.636}
    for name, (base, spread) in spreads.items():
        noise = np.random.default_rng([zlib.crc32(name.encode()), seed]).standard_normal(out[name].shape)
        drawn = base * np.exp(spread * noise) if base else spread * noise
        out[name] = jnp.asarray(drawn.astype(out[name].dtype))
    for name, factor in factors.items():
        out[name] = (out[name] * factor).astype(out[name].dtype)
    return out
```

```python
from contextlib import ExitStack

import numpy as np

import concourse.bass as bass
from concourse import mybir

F32 = mybir.dt.float32
F32R = mybir.dt.float32r
ALU = mybir.AluOpType
ACT = mybir.ActivationFunctionType
AX = mybir.AxisListType

P = 128
SAMPLES = 8
C = 256
CT = C // P
SIDE = 32
T = SIDE * SIDE
HALF = 512
NH = T // HALF
KT = T // P
D = 32
GROUP = 4
QT = HALF // P

PACK = []
for _l in "0123":
    PACK += [(f"wq{_l}", 512), (f"wk{_l}", 512), (f"wv{_l}", 512)]
    if _l != "1":
        PACK += [(f"wp{_l}", 512)]
PACK += [("mq", 512), ("mk", 512), ("mv", 512), ("ff1", 1024), ("ff2", 512), ("ffo", 512),
         ("sa1", 192), ("sa2", 96), ("sa3", 128), ("ident", P), ("gmean", P)]
for _n in ("0", "pre", "norm", "post", "2", "3"):
    PACK += [(f"gw{_n}", 2), (f"gb{_n}", 2)]
for _l in "023":
    PACK += [(f"bq{_l}", 2), (f"bk{_l}", 2), (f"bv{_l}", 2), (f"bp{_l}", 2)]
PACK += [("bsa1", 1), ("bsa2", 1), ("bsa3", 1), ("bff1", 2), ("bff2", 2), ("bffo", 2)]
AT = {}
_c = 0
for _n, _w in PACK:
    AT[_n] = (_c, _w)
    _c += _w
COLS = _c


class Attention:

    def __init__(self, name, wide, units, ctiles, scale, biased, lead, spread):
        self.name, self.wide, self.units, self.ctiles = name, wide, units, ctiles
        self.scale, self.biased = scale, biased
        self.lead, self.spread = lead, spread
        self.items = 4 if wide else KT
        self.tiles = 1 if wide else 2
        self.slots = self.items // 2 if wide else self.items
        self.maxima = 4 * NH if wide else GROUP * QT * NH
        self.steps = [(u, qh) for u in range(units) for qh in range(NH)] if wide else \
                     [(g, qh) for qh in range(NH) for g in range(units)]
        assert sum(lead) == sum(spread) == self.maxima


NARROW_LEAD, NARROW_SPREAD = [0, 0, 6, 6, 6, 14], [0, 5, 6, 6, 5, 5, 5, 0]
HEAD_SCALE = 1.0 / float(np.sqrt(D))
ATT0 = Attention("0", False, 2, 1, HEAD_SCALE, True, NARROW_LEAD, NARROW_SPREAD)
ATT1 = Attention("1", False, 2, 1, HEAD_SCALE, False, NARROW_LEAD, NARROW_SPREAD)
ATTM = Attention("m", True, 2, 1, 1.0 / float(np.sqrt(P)), False, [0, 0, 2, 2, 2, 2], [0, 4, 4, 0])
ATT2 = Attention("2", False, 2, 1, HEAD_SCALE, True, NARROW_LEAD, NARROW_SPREAD)
ATT3 = Attention("3", True, 1, 2, 1.0 / float(np.sqrt(C)), True, [0, 0, 0, 0, 4, 4], [0, 4, 4, 0])
LAYERS = (ATT0, ATT1, ATTM, ATT2, ATT3)
NORMS = 6

N_STEPS = sum(len(a.steps) for a in LAYERS)
N_TILES = sum(6 + len(a.steps) * a.items * a.tiles for a in LAYERS) + 3 * NH + 4 + 3 * NH
N_MX = sum(len(a.steps) * (a.maxima + 1 + a.wide) for a in LAYERS) + 2 * NORMS
N_SLOTS = sum(len(a.steps) * a.slots for a in LAYERS)
assert N_TILES % 2 == 0 and N_MX % 2 == 0
PER = {
    "tile_full": N_TILES, "tile_read0": N_TILES // 2, "tile_read1": N_TILES // 2,
    "mx_full": N_MX, "mx_read": N_MX,
    "p_used": N_SLOTS, "p_summed": sum(len(a.steps) * a.slots for a in LAYERS if a.wide),
    "acc_ready": sum(len(a.steps) for a in LAYERS if a.wide),
    "av_read": N_STEPS, "av_normed": N_STEPS, "nm_ready": N_STEPS, "row_ready": 16 * N_STEPS,
    "hi_ready": 4 * len(LAYERS),
    "stack_ready0": 16 * 3 * 24, "stack_ready1": 16 * 3 * 24,
    "gn_mean": NORMS, "gn_dev": NORMS, "gn_var": NORMS, "gn_rstd": NORMS,
    "act_ready": CT * 6, "x_loaded": 16, "pos_loaded": 16, "x_res_free": 16,
    "vec": 0,
}


class Count:

    def __init__(self, b):
        self.b, self.n = b, {}

    def next(self, name, k=1):
        self.n[name] = self.n.get(name, 0) + k
        return self.at(name, self.n[name])

    def at(self, name, n):
        return self.b * PER[name] + n

    def tile(self):
        self.n["tile"] = self.n.get("tile", -1) + 1
        return self.n["tile"]

    def tile_free(self, n):
        return self.at("tile_read0", n // 2)

    def tile_read(self, n):
        return self.at("tile_read0", n // 2 + 1)

    def tile_full(self, n):
        return self.at("tile_full", n + 1)

    def mx(self, k=1):
        self.n["mx"] = self.n.get("mx", -1) + k
        return self.n["mx"]


def build_program(nc, x, pos, pack, out, vec_per_sample):
    PER["vec"] = vec_per_sample
    ctx = ExitStack()
    with ctx:
        def sb(name, shape, dt=F32):
            return ctx.enter_context(nc.sbuf_tensor(name, shape, dt))

        W = sb("weights", [P, COLS])
        ONES = sb("ones", [P, P])
        ONEROW = sb("one_row", [1, P], F32R)
        POWER = sb("power", [P, 2])
        BOUT = sb("folded_bias", [P, 3, CT])
        X = sb("x_res", [P, CT, T])
        A = sb("act_a", [P, CT, T])
        H = sb("act_h", [P, CT, T])
        E = sb("act_e", [P, CT, T])
        AO = sb("att_out", [P, CT, T])
        QH = sb("q_hi", [P, 2, T], F32R)
        KH = sb("k_hi", [P, 2, T], F32R)
        VT = sb("v_tokens", [P, KT, C])
        QS = sb("q_stack", [P, NH, 2 * GROUP, HALF], F32R)
        KS = sb("k_stack", [P, 2 * GROUP, T], F32R)
        PR = sb("probs", [P, 2, 4, HALF])
        ACC = sb("probs_acc", [P, HALF])
        NOTE = sb("note", [P, 2])
        PAUSE = sb("pause", [P, 1])
        MC = sb("max_cols", [P, GROUP * QT, NH])
        NM = sb("neg_max", [P, GROUP * QT])
        NT_ = sb("neg_max_t", [GROUP * QT, P], F32R)
        AVS = sb("av_copy", [P, 2, HALF])
        RC = sb("recip", [P, HALF])
        ST = sb("stats", [P, CT, NH, 6])
        MV = sb("mean_var", [P, CT, 2])
        GM = sb("group_mean", [P, CT])
        DV = sb("deviation", [P, CT])
        SQ = sb("dev_squared", [P, CT])
        VV = sb("var_plus", [P, CT])
        VS = sb("group_var", [P, CT])
        VE = sb("var_eps", [P, CT])
        RS = sb("rstd", [P, CT])
        GA = sb("gn_scale", [P, CT])
        GB = sb("gn_shift", [P, CT])
        GT = sb("gn_shift_neg", [P, CT])
        S1 = sb("gate1", [3 * D, SIDE + 2, SIDE + 2])

        WT = [ctx.enter_context(nc.psum_tensor(f"work{i}", [P, 2, HALF], F32)) for i in range(2)]
        AVP = ctx.enter_context(nc.psum_tensor("av", [P, HALF], F32))
        AV2 = ctx.enter_context(nc.psum_tensor("av2_or_sums", [P, HALF], F32))
        MX = [ctx.enter_context(nc.psum_tensor(f"mx{i}", [P, HALF], F32)) for i in range(2)]

        PRF = PR[:, :, :, :].rearrange("p a b c -> p (a b c)")
        LO_NARROW = [PRF[:, i * T:(i + 1) * T].bitcast(F32R) for i in range(4)]
        QSF = QS[:, :, :, :].rearrange("p a h n -> p (a h n)")
        LO_WIDE = [QSF[:, i * T:(i + 1) * T] for i in range(4)]
        NR = QSF[0:1, 4 * T:5 * T].rearrange("o (a n) -> o a n", a=2)
        S2 = PRF[0:D, 0:T]

        S = {n: ctx.enter_context(nc.semaphore(n)) for n in PER}
        consts = ctx.enter_context(nc.semaphore("consts"))
        folded_mm = ctx.enter_context(nc.semaphore("folded_mm"))
        folded = ctx.enter_context(nc.semaphore("folded"))
        CONSTS = 6

        def w(name, parts=P):
            a, n = AT[name]
            return W[0:parts, a:a + n]

        def wcol(name, i, parts=P, base=0):
            a, _ = AT[name]
            return W[base:base + parts, a + i:a + i + 1]

        def read(slot):
            return S[f"tile_read{slot}"]

        block = ctx.enter_context(nc.Block())

        @block.sync
        def _(sp):
            sp.dma_start(H[:, :, :], x[0].rearrange("(t p) n -> p t n", p=P)).then_inc(S["x_loaded"], 16)
            sp.dma_start(W[:, :], pack).then_inc(S["x_res_free"], 16)
            sp.dma_start(E[:, :, :], pos.rearrange("(t p) n -> p t n", p=P)).then_inc(S["pos_loaded"], 16)
            with sp.Fori(0, SAMPLES) as b:
                c = Count(b)

                def stacks(att):
                    tiles = [c.tile() for _ in range(6)]
                    if att.wide:
                        return
                    for g in range(2):
                        sp.wait_ge(read(tiles[2 * g] % 2), c.tile_read(tiles[2 * g]))
                        sp.wait_ge(read(tiles[2 * g + 1] % 2), c.tile_read(tiles[2 * g + 1]))
                        done = S[f"stack_ready{g}"]
                        for j in range(GROUP):
                            h, rows = GROUP * g + j, slice(D * j, D * j + D)
                            q_hi, k_hi = QH[rows, g, :].bitcast(F32), KH[rows, g, :].bitcast(F32)
                            q_lo, k_lo = LO_NARROW[g][rows, :].bitcast(F32), LO_NARROW[2 + g][rows, :].bitcast(F32)
                            for i, part in enumerate((q_hi, q_lo, q_hi)):
                                sp.dma_start(QS[D * i:D * i + D, :, h, :].bitcast(F32),
                                             part.rearrange("p (a n) -> p a n", a=NH)).then_inc(done, 16)
                            for i, part in enumerate((k_hi, k_hi, k_lo)):
                                sp.dma_start(KS[D * i:D * i + D, h, :].bitcast(F32), part).then_inc(done, 16)

                def rows(att):
                    for u, qh in att.steps:
                        n = c.mx(att.maxima + 1)
                        sp.wait_ge(S["mx_read"], c.at("mx_read", n + 1))
                        sp.dma_start(QS[96:97, qh, GROUP * u:GROUP * u + GROUP, :]
                                     .rearrange("o h (a n) -> o (h a) n", n=P).bitcast(F32),
                                     NT_[:, :].bitcast(F32)).then_inc(S["row_ready"], 16)
                        for _ in range(att.items * att.tiles):
                            c.tile()

                def wide_rows(att):
                    steps = len(att.steps)
                    for s in range(steps):
                        if s >= 2:
                            c.mx(1)
                        n = c.mx(att.maxima + 1)
                        sp.wait_ge(S["mx_read"], c.at("mx_read", n + 1))
                        sp.dma_start(NR[0:1, s % 2, :].rearrange("o (a n) -> o a n", n=P).bitcast(F32),
                                     NT_[0:QT, :].bitcast(F32)).then_inc(S["row_ready"], 16)
                        for _ in range(att.items * att.tiles):
                            c.tile()
                    c.mx(min(2, steps))

                c.mx(2)
                stacks(ATT0)
                rows(ATT0)
                for _ in range(NH + 4):
                    c.tile()
                c.mx(4)
                stacks(ATT1)
                rows(ATT1)
                stacks(ATTM)
                wide_rows(ATTM)
                for _ in range(3 * NH):
                    n = c.tile()
                sp.wait_ge(read(n % 2), c.tile_read(n))
                sp.dma_start(H[:, :, :], x[(b + 1) % SAMPLES].rearrange("(t p) n -> p t n", p=P))\
                  .then_inc(S["x_loaded"], 16)
                sp.dma_start(E[:, :, :], pos.rearrange("(t p) n -> p t n", p=P)).then_inc(S["pos_loaded"], 16)
                c.mx(4)
                stacks(ATT2)
                rows(ATT2)
                for _ in range(NH):
                    c.tile()
                c.mx(2)
                stacks(ATT3)
                wide_rows(ATT3)
                for _ in range(NH):
                    n = c.tile()
                    sp.wait_ge(read(n % 2), c.tile_read(n))
                sp.dma_start(out[b].rearrange("(t p) n -> p t n", p=P), X[:, :, :]).then_inc(S["x_res_free"], 16)
            sp.wait_ge(S["x_res_free"], 16 * (SAMPLES + 1))
            sp.wait_ge(S["x_loaded"], 16 * (SAMPLES + 1))
            sp.wait_ge(S["pos_loaded"], 16 * (SAMPLES + 1))

        @block.gpsimd
        def _(pool):
            pool.memset(ONES[:, :], 1.0).then_inc(consts, 1)
            pool.memset(POWER[:, :], -0.5).then_inc(consts, 1)
            pool.memset(S1[:, :, :], 0.0).then_inc(consts, 1)
            for i, ones in enumerate((ONEROW[:, :], KS[96:97, 0:GROUP, :], KS[96:97, GROUP:, :])):
                pool.wait_ge(consts, 3 + i)
                pool.memset(ones.bitcast(F32), 1.0).then_inc(consts, 1)
            pool.wait_ge(consts, CONSTS)
            with pool.Fori(0, SAMPLES) as b:
                c = Count(b)
                for _ in range(NORMS):
                    pool.wait_ge(S["gn_var"], c.next("gn_var"))
                    pool.tensor_tensor(RS[:, :], VE[:, :], POWER[:, :], ALU.pow).then_inc(S["gn_rstd"], 1)

        @block.scalar
        def _(act):
            act.wait_ge(S["x_res_free"], 16)
            act.wait_ge(consts, CONSTS)
            with act.Fori(0, SAMPLES) as b:
                c = Count(b)
                slot = [0]
                steps = [0]
                summed = [0]

                def qkv(att):
                    for i in range(6):
                        n = c.tile()
                        act.wait_ge(S["tile_full"], c.tile_full(n))
                        src = WT[n % 2][:, :, :].rearrange("p a b -> p (a b)")
                        if i < 4:
                            g, dst, bias = i // 2, (QH, KH)[i % 2], ("bq", "bk")[i % 2]
                            if att.biased:
                                ins = act.activation(dst[:, g, :], src, ACT.Identity, bias=wcol(bias + att.name, g))
                            else:
                                ins = act.activation(dst[:, g, :], src, ACT.Identity)
                            ins.then_inc(S["hi_ready"], 1)
                        else:
                            k = 4 * (i - 4)
                            act.activation(VT[:, k:k + 4, :].rearrange("p a b -> p (a b)"), src, ACT.Identity)\
                               .then_inc(read(n % 2), 1)
                    if not att.wide:
                        for g in range(2):
                            act.wait_ge(S[f"stack_ready{g}"], c.next(f"stack_ready{g}", 16 * 24))

                def evacuate(att):
                    act.wait_ge(S["p_used"], c.at("p_used", slot_end[0]))
                    if steps[0]:
                        act.wait_ge(S["av_normed"], c.at("av_normed", steps[0]))
                    second = AV2 if (not att.wide or att.ctiles == 2) else None
                    if second is None:
                        act.activation(AVS[:, 0, :], AVP[:, :], ACT.Identity).then_inc(S["av_read"], 1)
                    else:
                        act.activation(AVS[:, 0, :], AVP[:, :], ACT.Identity)
                        act.activation(AVS[:, 1, :], second[:, :], ACT.Identity).then_inc(S["av_read"], 1)
                    steps[0] += 1

                slot_end = [0]

                def attention(att):
                    first_slot, first_sum = slot[0], summed[0]
                    for s in range(len(att.steps)):
                        for i in range(att.items):
                            for t in range(att.tiles):
                                half = i % 2 if att.wide else t
                                if half == 0 and slot[0] >= 2:
                                    act.wait_ge(S["p_used"], c.at("p_used", slot[0] - 1))
                                    if att.wide and slot[0] - first_slot >= 2:
                                        act.wait_ge(S["p_summed"], c.at("p_summed", summed[0] - 1))
                                n = c.tile()
                                act.wait_ge(S["tile_full"], c.tile_full(n))
                                act.activation(PR[:, slot[0] % 2, 2 * half:2 * half + 2, :], WT[n % 2][:, :, :],
                                               ACT.Exp, scale=att.scale).then_inc(read(n % 2), 1)
                                if half == 1:
                                    slot[0] += 1
                                    if att.wide:
                                        summed[0] += 1
                            if i == 0 and s > 0:
                                evacuate(att)
                        slot_end[0] = slot[0]
                    evacuate(att)

                for att in LAYERS:
                    qkv(att)
                    attention(att)
                    if att in (ATT0, ATT2, ATT3):
                        for _ in range(NH):
                            c.tile()
                    if att is ATT0:
                        n = c.tile()
                        act.wait_ge(S["tile_full"], c.tile_full(n))
                        for j in range(3):
                            ins = act.activation(
                                S1[D * j:D * j + D, 1:SIDE + 1, 2 - j:2 - j + SIDE],
                                WT[n % 2][D * j:D * j + D, :, :].rearrange("p a (r c) -> p (a r) c", c=SIDE),
                                ACT.Silu, bias=wcol("bsa1", 0, D, D * j))
                        ins.then_inc(read(n % 2), 1)
                        n = c.tile()
                        act.wait_ge(S["tile_full"], c.tile_full(n))
                        act.activation(S2[:, :], WT[n % 2][0:D, :, :].rearrange("p a b -> p (a b)"), ACT.Silu,
                                       bias=wcol("bsa2", 0, D)).then_inc(read(n % 2), 1)
                        for nh in range(NH):
                            n = c.tile()
                            act.wait_ge(S["tile_full"], c.tile_full(n))
                            act.activation(AO[:, 0, nh * HALF:(nh + 1) * HALF], WT[n % 2][:, 0, :], ACT.Sigmoid,
                                           bias=wcol("bsa3", 0)).then_inc(read(n % 2), 1)
                    if att is ATTM:
                        for dst, bias, func in ((H, "bff1", ACT.Silu), (E, "bff2", ACT.Identity),
                                                (A, "bffo", ACT.Identity)):
                            for nh in range(NH):
                                n = c.tile()
                                act.wait_ge(S["tile_full"], c.tile_full(n))
                                for m in range(CT):
                                    ins = act.activation(dst[:, m, nh * HALF:(nh + 1) * HALF], WT[n % 2][:, m, :],
                                                         func, bias=wcol(bias, m))
                                ins.then_inc(read(n % 2), 1)

        @block.vector
        def _(dve):
            dve.wait_ge(S["x_res_free"], 16)
            dve.wait_ge(folded_mm, 1)
            for i, l in enumerate("023"):
                ins = dve.tensor_tensor(BOUT[:, i, :], MX[0][:, CT * i:CT * i + CT], w(f"bp{l}"), ALU.add)
            ins.then_inc(folded, 1)
            dve.wait_ge(folded, 1)
            total = {}
            with dve.Fori(0, SAMPLES) as b:
                c = Count(b)

                def chain(ins):
                    ins.then_inc(S["vec"], 1)
                    dve.wait_ge(S["vec"], c.next("vec"))

                def norm(src, name, eps, apply):
                    for t in range(CT):
                        for nh in range(NH):
                            ins = dve.bn_stats(ST[:, t, nh, :], src[:, t, nh * HALF:(nh + 1) * HALF])
                    chain(ins)
                    dve.memset(PAUSE[:, :], 0.0)
                    for t in range(CT):
                        ins = dve.bn_aggr(MV[:, t, :], ST[:, t, :, :].rearrange("p a b -> p (a b)"))
                    ins.then_inc(S["gn_mean"], 1)
                    dve.wait_ge(S["gn_mean"], c.next("gn_mean"))
                    n = c.mx()
                    dve.wait_ge(S["mx_full"], c.at("mx_full", n + 1))
                    dve.tensor_copy(GM[:, :], MX[n % 2][:, 0:CT]).then_inc(S["mx_read"], 1)
                    dve.wait_ge(S["mx_read"], c.at("mx_read", n + 1))
                    chain(dve.tensor_tensor(DV[:, :], MV[:, :, 0], GM[:, :], ALU.subtract))
                    chain(dve.tensor_tensor(SQ[:, :], DV[:, :], DV[:, :], ALU.mult))
                    dve.tensor_tensor(VV[:, :], SQ[:, :], MV[:, :, 1], ALU.add).then_inc(S["gn_dev"], 1)
                    n = c.mx()
                    dve.wait_ge(S["mx_full"], c.at("mx_full", n + 1))
                    dve.tensor_copy(VS[:, :], MX[n % 2][:, 0:CT]).then_inc(S["mx_read"], 1)
                    dve.wait_ge(S["mx_read"], c.at("mx_read", n + 1))
                    dve.tensor_scalar(VE[:, :], VS[:, :], eps, None, ALU.add).then_inc(S["gn_var"], 1)
                    dve.wait_ge(S["gn_rstd"], c.next("gn_rstd"))
                    chain(dve.tensor_tensor(GA[:, :], RS[:, :], w(f"gw{name}"), ALU.mult))
                    chain(dve.tensor_tensor(GT[:, :], GM[:, :], GA[:, :], ALU.mult))
                    chain(dve.tensor_tensor(GB[:, :], w(f"gb{name}"), GT[:, :], ALU.subtract))
                    for t in range(CT):
                        apply(t, GA[:, t:t + 1], GB[:, t:t + 1])

                def apply_to(src, dst):
                    def apply(t, scale, shift):
                        dve.tensor_scalar(dst[:, t, :], src[:, t, :], scale, shift, ALU.mult, ALU.add)\
                           .then_inc(S["act_ready"], 1)
                        c.next("act_ready")
                    return apply

                def maxima(att, k):
                    for _ in range(k):
                        n = c.mx()
                        i = mi[0]
                        mi[0] += 1
                        dve.wait_ge(S["mx_full"], c.at("mx_full", n + 1))
                        if att.wide:
                            col, kh = i // NH, i % NH
                        else:
                            qt, kh, j = i // (NH * GROUP), i // GROUP % NH, i % GROUP
                            col = j * QT + qt
                        dve.tensor_reduce(MC[:, col, kh:kh + 1], MX[n % 2][:, :], AX.X, ALU.max)\
                           .then_inc(S["mx_read"], 1)
                    if mi[0] == att.maxima and k:
                        cols = QT if att.wide else GROUP * QT
                        dve.wait_ge(S["mx_read"], c.at("mx_read", n + 1))
                        dve.tensor_reduce(NM[:, 0:cols], MC[:, 0:cols, :], AX.X, ALU.max, negate=True)\
                           .then_inc(S["nm_ready"], 1)
                        c.next("nm_ready")

                mi = [0]

                def columns(att):
                    cols = QT if att.wide else GROUP * QT
                    n = c.mx()
                    if c.n.get("row_ready"):
                        dve.wait_ge(S["row_ready"], c.at("row_ready", c.n["row_ready"]))
                    dve.wait_ge(S["mx_full"], c.at("mx_full", n + 1))
                    dve.tensor_copy(NT_[0:cols, :], MX[n % 2][0:cols, 0:P]).then_inc(S["mx_read"], 1)
                    c.next("row_ready", 16)
                    mi[0] = 0

                def qkv(att):
                    los = LO_WIDE if att.wide else LO_NARROW
                    for i in range(6):
                        n = c.tile()
                        if i < 4:
                            g, hi, bias = i // 2, (QH, KH)[i % 2], ("bq", "bk")[i % 2]
                            dve.wait_ge(S["hi_ready"], c.next("hi_ready"))
                            dve.scalar_tensor_tensor(
                                out=los[2 * (i % 2) + g], in0=WT[n % 2][:, :, :].rearrange("p a b -> p (a b)"),
                                scalar=wcol(bias + att.name, g) if att.biased else 0.0,
                                in1=hi[:, g, :].bitcast(F32), op0=ALU.add, op1=ALU.subtract)\
                                .then_inc(read(n % 2), 1)
                        maxima(att, att.lead[i])
                    columns(att)

                def normalize(att, s, dst):
                    u, qh = att.steps[s]
                    cols = slice(qh * HALF, (qh + 1) * HALF)
                    if att.wide:
                        n = c.mx()
                        dve.wait_ge(S["mx_full"], c.at("mx_full", n + 1))
                        dve.reciprocal(RC[:, :], MX[n % 2][:, :]).then_inc(S["mx_read"], 1)
                        dve.wait_ge(S["mx_read"], c.at("mx_read", n + 1))
                        dve.wait_ge(S["av_read"], c.next("av_read"))
                    else:
                        dve.wait_ge(S["av_read"], c.next("av_read"))
                        chain(dve.reciprocal(RC[:, :], AVS[:, 1, :]))
                    for d in range(att.ctiles):
                        ins = dve.tensor_tensor(dst[:, u + d, cols], AVS[:, d, :], RC[:, :], ALU.mult)
                    ins.then_inc(S["av_normed"], 1)

                def accumulate(att, i):
                    n = c.tile()
                    dve.wait_ge(read(n % 2), c.tile_read(n))
                    half, m = i % 2, wide_slot[0]
                    for jj in range(2):
                        pt = PR[:, m % 2, 2 * half + jj, :]
                        if i == 0 and jj == 0:
                            continue
                        prev = PR[:, m % 2, 0, :] if i == 0 else ACC[:, :]
                        ins = dve.tensor_tensor(ACC[:, :], prev, pt, ALU.add)
                        if i == att.items - 1 and jj == 1:
                            chain(ins)
                            dve.tensor_copy(NOTE[:, 0:1], ACC[:, 0:1]).then_inc(S["acc_ready"], 1)
                            dve.tensor_copy(NOTE[:, 1:2], ACC[:, 0:1]).then_inc(S["p_summed"], 1)
                        elif half == 1 and jj == 1:
                            ins.then_inc(S["p_summed"], 1)
                            dve.wait_ge(S["p_summed"], c.at("p_summed", c.n.get("p_summed", 0) + 1))
                        else:
                            chain(ins)
                    if half == 1:
                        c.next("p_summed")
                        wide_slot[0] += 1

                wide_slot = [0]

                def attention(att, dst):
                    wide_slot[0] = 0
                    steps = len(att.steps)
                    for s in range(steps):
                        for i in range(att.items):
                            if s + 1 < steps:
                                maxima(att, att.spread[i])
                                if i == att.items - 1:
                                    columns(att)
                            if s > 0 and i == (0 if att.wide else 1):
                                normalize(att, s - 1, dst)
                            if att.wide:
                                accumulate(att, i)
                            else:
                                c.tile()
                                c.tile()
                    normalize(att, steps - 1, dst)

                def project(i, residual):
                    for nh in range(NH):
                        n = c.tile()
                        dve.wait_ge(S["tile_full"], c.tile_full(n))
                        for m in range(CT):
                            cols = slice(nh * HALF, (nh + 1) * HALF)
                            ins = dve.scalar_tensor_tensor(out=X[:, m, cols], in0=WT[n % 2][:, m, :],
                                                           scalar=BOUT[:, i, m:m + 1], in1=residual[:, m, cols],
                                                           op0=ALU.add, op1=ALU.add)
                        ins.then_inc(read(n % 2), 1)
                    dve.wait_ge(read(n % 2), c.tile_read(n))

                dve.wait_ge(S["x_loaded"], c.next("x_loaded", 16))
                norm(H, "0", 1e-5, apply_to(H, A))
                qkv(ATT0)
                attention(ATT0, AO)
                dve.wait_ge(S["x_res_free"], c.next("x_res_free", 16))
                project(0, H)

                def apply_pre(t, scale, shift):
                    chain(dve.tensor_scalar(A[:, t, :], X[:, t, :], scale, shift, ALU.mult, ALU.add))
                    dve.tensor_tensor(A[:, t, :], A[:, t, :], E[:, t, :], ALU.add).then_inc(S["act_ready"], 1)
                    c.next("act_ready")
                    dve.wait_ge(S["act_ready"], c.at("act_ready", c.n["act_ready"]))

                dve.wait_ge(S["pos_loaded"], c.next("pos_loaded", 16))
                norm(X, "pre", 1e-6, apply_pre)
                norm(A, "norm", 1e-6, apply_to(A, H))
                for _ in range(2):
                    c.tile()
                for nh in range(NH):
                    n = c.tile()
                    dve.wait_ge(read(n % 2), c.tile_read(n))
                for t in range(CT):
                    dve.tensor_tensor(E[:, t, :], A[:, t, :], AO[:, 0, :], ALU.mult).then_inc(S["act_ready"], 1)
                    c.next("act_ready")
                dve.wait_ge(S["act_ready"], c.at("act_ready", c.n["act_ready"]))
                qkv(ATT1)
                attention(ATT1, AO)
                qkv(ATTM)
                attention(ATTM, A)
                for _ in range(2 * NH):
                    c.tile()
                for nh in range(NH):
                    n = c.tile()
                    dve.wait_ge(read(n % 2), c.tile_read(n))

                def apply_post(t, scale, shift):
                    chain(dve.scalar_tensor_tensor(out=X[:, t, :], in0=A[:, t, :], scalar=scale, in1=X[:, t, :],
                                                   op0=ALU.mult, op1=ALU.add))
                    chain(dve.tensor_scalar(X[:, t, :], X[:, t, :], shift, None, ALU.add))

                norm(A, "post", 1e-6, apply_post)

                norm(X, "2", 1e-5, apply_to(X, A))
                qkv(ATT2)
                attention(ATT2, AO)
                project(1, A)

                norm(X, "3", 1e-5, apply_to(X, A))
                qkv(ATT3)
                attention(ATT3, AO)
                project(2, X)
                total.update(c.n)
            assert total["vec"] == PER["vec"], f"vec {total['vec']}"
            assert total["act_ready"] == PER["act_ready"], total
            assert total["tile"] + 1 == N_TILES and total["mx"] + 1 == N_MX, (total, N_TILES, N_MX)

        @block.tensor
        def _(pe):
            def mm(dst, lhsT, rhs, start, stop, **kw):
                return nc.tensor.matmul(dst, lhsT, rhs, start=start, stop=stop, **kw)

            pe.wait_ge(S["x_res_free"], 16)
            pe.wait_ge(consts, CONSTS)
            for i, l in enumerate("023"):
                wp = w(f"wp{l}").rearrange("p (k n) -> p k n", k=CT)
                for m in range(CT):
                    for k in range(CT):
                        ins = mm(MX[0][:, CT * i + m:CT * i + m + 1], wp[:, k, m * P:(m + 1) * P],
                                 wcol(f"bv{l}", k), k == 0, k == CT - 1)
            ins.then_inc(folded_mm, 1)
            pe.wait_ge(folded, 1)
            total = {}
            with pe.Fori(0, SAMPLES) as b:
                c = Count(b)

                def new_tile():
                    n = c.tile()
                    if n >= 2:
                        pe.wait_ge(read(n % 2), c.tile_free(n))
                    return n, WT[n % 2]

                def new_bank():
                    n = c.mx()
                    if n >= 2:
                        pe.wait_ge(S["mx_read"], c.at("mx_read", n - 1))
                    return MX[n % 2]

                def group_means():
                    bank = new_bank()
                    pe.wait_ge(S["gn_mean"], c.next("gn_mean"))
                    mm(bank[:, 0:CT], w("gmean"), MV[:, :, 0], True, True).then_inc(S["mx_full"], 1)
                    bank = new_bank()
                    pe.wait_ge(S["gn_dev"], c.next("gn_dev"))
                    mm(bank[:, 0:CT], w("gmean"), VV[:, :], True, True).then_inc(S["mx_full"], 1)

                mi = [0]

                def maxima(att, s, k):
                    u, qh = att.steps[s]
                    for _ in range(k):
                        i = mi[0]
                        mi[0] += 1
                        bank = new_bank()
                        if att.wide:
                            qt, kh = i // NH, i % NH
                            q0 = qh * HALF + qt * P
                            for ct in range(att.ctiles):
                                ins = mm(bank[:, :], QH[:, u + ct, q0:q0 + P],
                                         KH[:, u + ct, kh * HALF:(kh + 1) * HALF], ct == 0, ct == att.ctiles - 1)
                        else:
                            qt, kh, j = i // (NH * GROUP), i // GROUP % NH, i % GROUP
                            q0 = qh * HALF + qt * P
                            r = slice(D * j, D * j + D)
                            ins = mm(bank[:, :], QH[r, u, q0:q0 + P], KH[r, u, kh * HALF:(kh + 1) * HALF], True, True,
                                     tile_position=(D * j, 0))
                        ins.then_inc(S["mx_full"], 1)

                def columns(att):
                    cols = QT if att.wide else GROUP * QT
                    bank = new_bank()
                    pe.wait_ge(S["nm_ready"], c.next("nm_ready"))
                    nc.tensor.transpose(bank[0:cols, 0:P], NM[:, 0:cols], w("ident")).then_inc(S["mx_full"], 1)
                    mi[0] = 0

                def qkv(att, src_q, src_kv, wq, wk, wv):
                    tiles = []
                    for i in range(6):
                        n, tile = new_tile()
                        tiles.append(n)
                        if i < 4:
                            g, src, wt = i // 2, (src_q, src_kv)[i % 2], w((wq, wk)[i % 2])
                            wt = wt.rearrange("p (g k n) -> p g k n", g=2, k=CT)
                            for nh in range(NH):
                                for k in range(CT):
                                    ins = mm(tile[:, nh, :], wt[:, g, k, :], src[:, k, nh * HALF:(nh + 1) * HALF],
                                             k == 0, k == CT - 1)
                        else:
                            wt = w(wv).rearrange("p (k n) -> p k n", k=CT)
                            for t in range(4):
                                tok = (4 * (i - 4) + t) * P
                                for k in range(CT):
                                    ins = mm(tile[:, t // 2, t % 2 * C:(t % 2 + 1) * C], src_kv[:, k, tok:tok + P],
                                             wt[:, k, :], k == 0, k == CT - 1)
                        ins.then_inc(S["tile_full"], 1)
                        if att.lead[i]:
                            if mi[0] == 0:
                                for t in tiles[2:4] if att.ctiles == 2 else tiles[:2]:
                                    pe.wait_ge(read(t % 2), c.tile_read(t))
                            maxima(att, 0, att.lead[i])
                    columns(att)
                    for t in tiles[4:]:
                        pe.wait_ge(read(t % 2), c.tile_read(t))
                    if not att.wide:
                        for g in range(2):
                            pe.wait_ge(S[f"stack_ready{g}"], c.next(f"stack_ready{g}", 16 * 24))

                def scores(att, s, i):
                    u, qh = att.steps[s]
                    qs = slice(qh * HALF, (qh + 1) * HALF)
                    made = []
                    for t in range(att.tiles):
                        n, tile = new_tile()
                        made.append(n)
                        for jj in range(2):
                            if att.wide:
                                ks = slice((2 * i + jj) * P, (2 * i + jj + 1) * P)
                                for ct in range(att.ctiles):
                                    kh, kl = KH[:, u + ct, ks], LO_WIDE[2 + u + ct][:, ks]
                                    qh_, ql = QH[:, u + ct, qs], LO_WIDE[u + ct][:, qs]
                                    mm(tile[:, jj, :], kh, qh_, ct == 0, False)
                                    mm(tile[:, jj, :], kh, ql, False, False)
                                    mm(tile[:, jj, :], kl, qh_, False, False)
                                ins = mm(tile[:, jj, :], ONEROW[:, :], NR[0:1, s % 2, :], False, True)
                            else:
                                h = GROUP * u + 2 * t + jj
                                ins = mm(tile[:, jj, :], KS[0:97, h, i * P:(i + 1) * P], QS[0:97, qh, h, :], True, True)
                        ins.then_inc(S["tile_full"], 1)
                    return made

                slot = [0]
                step = [0]

                def values(att, s, i, made):
                    u, _ = att.steps[s]
                    for n in made:
                        pe.wait_ge(read(n % 2), c.tile_read(n))
                    if i == 0:
                        if step[0]:
                            pe.wait_ge(S["av_read"], c.at("av_read", step[0]))
                        step[0] += 1
                    pt = PR[:, slot[0] % 2, :, :]
                    if att.wide:
                        for jj in range(2):
                            kt = 2 * i + jj
                            for d in range(att.ctiles):
                                col = (u + d) * P
                                ins = mm((AVP, AV2)[d][:, :], VT[:, kt, col:col + P], pt[:, 2 * (i % 2) + jj, :],
                                         kt == 0, kt == KT - 1)
                        if i % 2 == 1:
                            ins.then_inc(S["p_used"], 1)
                            slot[0] += 1
                    else:
                        for j in range(GROUP):
                            h = GROUP * u + j
                            mm(AVP[D * j:D * j + D, :], VT[:, i, D * h:D * h + D], pt[:, j, :], i == 0, i == KT - 1,
                               tile_position=(0, D * j))
                        for j in range(GROUP):
                            ins = mm(AV2[D * j:D * j + D, :], ONES[:, 0:D], pt[:, j, :], i == 0, i == KT - 1,
                                     tile_position=(0, D * j))
                        ins.then_inc(S["p_used"], 1)
                        slot[0] += 1
                    if att.wide and i == att.items - 1:
                        bank = new_bank()
                        pe.wait_ge(S["acc_ready"], c.next("acc_ready"))
                        mm(bank[:, :], ONES[:, :], ACC[:, :], True, True).then_inc(S["mx_full"], 1)

                def attention(att):
                    behind = None
                    for s in range(len(att.steps)):
                        for i in range(att.items):
                            if i == 0:
                                pe.wait_ge(S["row_ready"], c.next("row_ready", 16))
                            made = scores(att, s, i)
                            if s + 1 < len(att.steps):
                                maxima(att, s + 1, att.spread[i])
                            if behind is not None:
                                values(att, *behind)
                            if s + 1 < len(att.steps) and i == att.items - 1:
                                columns(att)
                            behind = (s, i, made)
                    values(att, *behind)

                def dense(srcs, weights, ready):
                    wt = w(weights).rearrange("p (k n) -> p k n", n=C)
                    made = []
                    for nh in range(NH):
                        n, tile = new_tile()
                        if nh == 0:
                            ready()
                        made.append(n)
                        for m in range(CT):
                            for k in range(CT * len(srcs)):
                                ins = mm(tile[:, m, :], wt[:, k, m * P:(m + 1) * P],
                                         srcs[k // CT][:, k % CT, nh * HALF:(nh + 1) * HALF],
                                         k == 0, k == CT * len(srcs) - 1)
                        ins.then_inc(S["tile_full"], 1)
                    return made

                def normed():
                    pe.wait_ge(S["av_normed"], c.at("av_normed", step[0]))

                def wait_tiles(made):
                    def ready():
                        for n in made:
                            pe.wait_ge(read(n % 2), c.tile_read(n))
                    return ready

                group_means()
                pe.wait_ge(S["act_ready"], c.next("act_ready", 2))
                qkv(ATT0, A, A, "wq0", "wk0", "wv0")
                attention(ATT0)
                dense([AO], "wp0", normed)

                group_means()
                n, tile = new_tile()
                pe.wait_ge(S["act_ready"], c.next("act_ready", 2))
                w1 = w("sa1").rearrange("p (k n) -> p k n", k=CT)
                for nh in range(NH):
                    for k in range(CT):
                        ins = mm(tile[0:3 * D, nh, :], w1[:, k, :], A[:, k, nh * HALF:(nh + 1) * HALF],
                                 k == 0, k == CT - 1)
                ins.then_inc(S["tile_full"], 1)
                group_means()
                pe.wait_ge(read(n % 2), c.tile_read(n))
                n, tile = new_tile()
                w2 = w("sa2", 3 * D).rearrange("p (k n) -> p k n", k=3)
                rows = SIDE // NH
                for nh in range(NH):
                    for dy in range(3):
                        ins = mm(tile[0:D, nh, :], w2[:, dy, :],
                                 S1[:, dy + rows * nh:dy + rows * (nh + 1), 1:SIDE + 1], dy == 0, dy == 2)
                ins.then_inc(S["tile_full"], 1)
                pe.wait_ge(read(n % 2), c.tile_read(n))
                for nh in range(NH):
                    n, tile = new_tile()
                    mm(tile[:, 0, :], w("sa3", D), S2[:, nh * HALF:(nh + 1) * HALF], True, True)\
                        .then_inc(S["tile_full"], 1)
                pe.wait_ge(S["act_ready"], c.next("act_ready", 2))
                qkv(ATT1, H, H, "wq1", "wk1", "wv1")
                attention(ATT1)
                pe.wait_ge(S["act_ready"], c.next("act_ready", 2))
                qkv(ATTM, E, H, "mq", "mk", "mv")
                attention(ATTM)
                made = dense([AO, A], "ff1", normed)
                made = dense([H], "ff2", wait_tiles(made))
                dense([E], "ffo", wait_tiles(made))
                group_means()

                group_means()
                pe.wait_ge(S["act_ready"], c.next("act_ready", 2))
                qkv(ATT2, A, A, "wq2", "wk2", "wv2")
                attention(ATT2)
                dense([AO], "wp2", normed)

                group_means()
                pe.wait_ge(S["act_ready"], c.next("act_ready", 2))
                qkv(ATT3, A, A, "wq3", "wk3", "wv3")
                attention(ATT3)
                dense([AO], "wp3", normed)
                total.update(c.n)
            assert total["tile"] + 1 == N_TILES and total["mx"] + 1 == N_MX, (total, N_TILES, N_MX)


def lay_out(a):
    f = np.float32

    def rows(m, order):
        return np.asarray(m)[order]

    def stationary(m):
        return np.asarray(m).reshape(2, P, CT, P).transpose(3, 0, 2, 1).reshape(P, -1)

    def moving(m):
        m = np.asarray(m)
        return m.reshape(m.shape[0], -1, P).transpose(2, 1, 0).reshape(P, -1)

    def cols(v):
        return np.asarray(v).reshape(CT, P).T

    def padded(m):
        m = np.asarray(m)
        return np.concatenate([m, np.zeros((P - m.shape[0], m.shape[1]), f)])

    heads = np.arange(3 * C).reshape(C // D, 3, D)
    split = [heads[:, i].reshape(-1) for i in range(3)]
    plain = [np.arange(C) + i * C for i in range(3)]
    v = {}
    for l, order, proj in (("0", split, "proj"), ("2", split, "proj"), ("3", plain, "out")):
        wt, bs = a[f"L{l}_conv_qkv_w"], a[f"L{l}_conv_qkv_b"]
        v[f"wq{l}"], v[f"wk{l}"] = (stationary(rows(wt, order[i])) for i in range(2))
        v[f"wv{l}"] = moving(rows(wt, order[2]))
        v[f"wp{l}"] = moving(a[f"L{l}_conv_{proj}_w"])
        for i, n in enumerate(("bq", "bk", "bv")):
            v[f"{n}{l}"] = cols(rows(bs, order[i]))
        v[f"bp{l}"] = cols(a[f"L{l}_conv_{proj}_b"])
        v[f"gw{l}"], v[f"gb{l}"] = cols(a[f"L{l}_conv_gn_w"]), cols(a[f"L{l}_conv_gn_b"])
    one = {k[8:]: np.asarray(x) for k, x in a.items() if k.startswith("L1_conv_")}
    v["wq1"], v["wk1"], v["wv1"] = stationary(one["wq"]), stationary(one["wk"]), moving(one["wv"])
    v["mq"] = stationary(np.concatenate([one["wq0"], one["wq1"]]))
    v["mk"] = stationary(np.concatenate([one["wk0"], one["wk1"]]))
    v["mv"] = moving(np.concatenate([one["wv0"], one["wv1"]]))
    v["ff1"], v["ff2"], v["ffo"] = moving(one["ff_w1"]), moving(one["ff_w2"]), moving(one["out_w"])
    v["sa1"] = moving(np.tile(one["sa_w1"].reshape(D, C), (3, 1)))
    v["sa2"] = padded(one["sa_w2"].transpose(3, 1, 2, 0).reshape(3 * D, 3 * D))
    v["sa3"] = padded(np.tile(one["sa_w3"].reshape(1, D), (P, 1)).T)
    v["ident"] = np.eye(P, dtype=f)
    v["gmean"] = np.kron(np.eye(P // 8, dtype=f), np.full((8, 8), 1 / 8, f))
    for n in ("pre", "norm", "post"):
        v[f"gw{n}"], v[f"gb{n}"] = cols(one[f"{n}_g"]), cols(one[f"{n}_b"])
    v["bsa1"] = padded(np.tile(one["sa_b1"], 3)[:, None])
    v["bsa2"] = padded(one["sa_b2"][:, None])
    v["bsa3"] = np.tile(one["sa_b3"], P)[:, None]
    v["bff1"], v["bff2"], v["bffo"] = cols(one["ff_b1"]), cols(one["ff_b2"]), cols(one["out_b"])
    for n, width in PACK:
        assert v[n].shape == (P, width), (n, v[n].shape)
    return np.ascontiguousarray(np.concatenate([v[n] for n, _ in PACK], axis=1))


def kernel(**inputs):
    import concourse.bacc as bacc
    from concourse.bass_utils import run_bass_kernel_spmd

    arrays = {
        "x_dram": np.ascontiguousarray(inputs["x"]).reshape(SAMPLES, C, T),
        "pos_dram": np.ascontiguousarray(inputs["L1_conv_pos_emb"]).reshape(C, T),
        "pack_dram": lay_out(inputs),
    }
    nc = bacc.Bacc("TRN2", target_bir_lowering=False, num_devices=1)
    args = [nc.dram_tensor(n, v.shape, F32, kind="ExternalInput").ap() for n, v in arrays.items()]
    out = nc.dram_tensor("out_dram", (SAMPLES, C, T), F32, kind="ExternalOutput").ap()
    build_program(nc, *args, out, VEC)
    r = run_bass_kernel_spmd(nc, [arrays], core_ids=[0])
    return r.results[0]["out_dram"].reshape(SAMPLES, C, SIDE, SIDE)


VEC = 90
```

```python
from contextlib import ExitStack

import numpy as np

import concourse.bass as bass
from concourse import mybir

F32 = mybir.dt.float32
F32R = mybir.dt.float32r
ALU = mybir.AluOpType
ACT = mybir.ActivationFunctionType
AX = mybir.AxisListType

P = 128
SAMPLES = 8
C = 256
CT = C // P
SIDE = 32
T = SIDE * SIDE
HALF = 512
NH = T // HALF
KT = T // P
D = 32
GROUP = 4
QT = HALF // P

PACK = []
for _l in "0123":
    PACK += [(f"wq{_l}", 512), (f"wk{_l}", 512), (f"wv{_l}", 512)]
    if _l != "1":
        PACK += [(f"wp{_l}", 512)]
PACK += [("mq", 512), ("mk", 512), ("mv", 512), ("ff1", 1024), ("ff2", 512), ("ffo", 512),
         ("sa1", 192), ("sa2", 96), ("sa3", 128), ("ident", P), ("gmean", P)]
for _n in ("0", "pre", "norm", "post", "2", "3"):
    PACK += [(f"gw{_n}", 2), (f"gb{_n}", 2)]
for _l in "023":
    PACK += [(f"bq{_l}", 2), (f"bk{_l}", 2), (f"bv{_l}", 2), (f"bp{_l}", 2)]
PACK += [("bsa1", 1), ("bsa2", 1), ("bsa3", 1), ("bff1", 2), ("bff2", 2), ("bffo", 2)]
AT = {}
_c = 0
for _n, _w in PACK:
    AT[_n] = (_c, _w)
    _c += _w
COLS = _c


class Attention:

    def __init__(self, name, wide, units, ctiles, scale, biased, lead, spread):
        self.name, self.wide, self.units, self.ctiles = name, wide, units, ctiles
        self.scale, self.biased = scale, biased
        self.lead, self.spread = lead, spread
        self.items = 4 if wide else KT
        self.tiles = 1 if wide else 2
        self.slots = self.items // 2 if wide else self.items
        self.maxima = 4 * NH if wide else GROUP * QT * NH
        self.steps = [(u, qh) for u in range(units) for qh in range(NH)] if wide else \
                     [(g, qh) for qh in range(NH) for g in range(units)]
        assert sum(lead) == sum(spread) == self.maxima

    def pairs(self, s):
        return PAIRS if s + 1 < len(self.steps) and not self.wide else 0


NARROW_LEAD, NARROW_SPREAD = [0, 0, 0, 8, 8, 16], [5, 4, 4, 5, 4, 5, 5, 0]
PAIRS = 3
P_RING = 3
HEAD_SCALE = 1.0 / float(np.sqrt(D))
ATT0 = Attention("0", False, 2, 1, HEAD_SCALE, True, NARROW_LEAD, NARROW_SPREAD)
ATT1 = Attention("1", False, 2, 1, HEAD_SCALE, False, NARROW_LEAD, NARROW_SPREAD)
ATTM = Attention("m", True, 2, 1, 1.0 / float(np.sqrt(P)), False, [0, 0, 2, 2, 2, 2], [0, 4, 4, 0])
ATT2 = Attention("2", False, 2, 1, HEAD_SCALE, True, NARROW_LEAD, NARROW_SPREAD)
ATT3 = Attention("3", True, 1, 2, 1.0 / float(np.sqrt(C)), True, [0, 0, 0, 0, 4, 4], [0, 4, 4, 0])
LAYERS = (ATT0, ATT1, ATTM, ATT2, ATT3)
NORMS = 6

N_STEPS = sum(len(a.steps) for a in LAYERS)
N_TILES = sum(6 + len(a.steps) * a.items * a.tiles for a in LAYERS) + 3 * NH + 4 + 3 * NH
N_MX = sum(len(a.steps) * (a.maxima + 1 + a.wide) for a in LAYERS) + 2 * NORMS
N_SLOTS = sum(len(a.steps) * a.slots for a in LAYERS)
assert N_TILES % 2 == 0 and N_MX % 2 == 0 and N_SLOTS % P_RING == 0
PER = {
    "tile_full": N_TILES, "tile_read0": N_TILES // 2, "tile_read1": N_TILES // 2,
    "mx_full": N_MX, "mx_read": N_MX,
    "p_used": N_SLOTS, "p_summed": sum(len(a.steps) * a.slots for a in LAYERS if a.wide),
    "pair_ready": sum(a.pairs(s) for a in LAYERS for s in range(len(a.steps))),
    "pair_used": sum(a.pairs(s) for a in LAYERS for s in range(len(a.steps))), "border": 1,
    "acc_ready": sum(len(a.steps) for a in LAYERS if a.wide),
    "av_read": N_STEPS, "av_normed": N_STEPS, "nm_ready": N_STEPS, "row_ready": 16 * N_STEPS,
    "hi_ready": 4 * len(LAYERS),
    "stack_ready0": 16 * 3 * 24, "stack_ready1": 16 * 3 * 24,
    "gn_mean": NORMS, "gn_dev": NORMS, "gn_var": NORMS, "gn_rstd": NORMS,
    "act_ready": CT * 6, "x_loaded": 16, "pos_loaded": 16, "x_res_free": 16,
    "vec": 0,
}


class Count:

    def __init__(self, b):
        self.b, self.n = b, {}

    def next(self, name, k=1):
        self.n[name] = self.n.get(name, 0) + k
        return self.at(name, self.n[name])

    def at(self, name, n):
        return self.b * PER[name] + n

    def tile(self):
        self.n["tile"] = self.n.get("tile", -1) + 1
        return self.n["tile"]

    def tile_free(self, n):
        return self.at("tile_read0", n // 2)

    def tile_read(self, n):
        return self.at("tile_read0", n // 2 + 1)

    def tile_full(self, n):
        return self.at("tile_full", n + 1)

    def mx(self, k=1):
        self.n["mx"] = self.n.get("mx", -1) + k
        return self.n["mx"]


def build_program(nc, x, pos, pack, out, vec_per_sample):
    PER["vec"] = vec_per_sample
    ctx = ExitStack()
    with ctx:
        def sb(name, shape, dt=F32):
            return ctx.enter_context(nc.sbuf_tensor(name, shape, dt))

        W = sb("weights", [P, COLS])
        ONES = sb("ones", [P, P])
        ONEROW = sb("one_row", [1, P], F32R)
        POWER = sb("power", [P, 2])
        BOUT = sb("folded_bias", [P, 3, CT])
        X = sb("x_res", [P, CT, T])
        A = sb("act_a", [P, CT, T])
        H = sb("act_h", [P, CT, T])
        E = sb("act_e", [P, CT, T])
        AO = sb("att_out", [P, CT, T])
        Q0 = sb("q_hi0", [P, T], F32R)
        K0 = sb("k_hi0", [P, T], F32R)
        VT = sb("v_tokens", [P, KT, C])
        QS = sb("q_stack", [P, NH, 2 * GROUP, HALF], F32R)
        KS = sb("k_stack", [P, 2 * GROUP, T], F32R)
        PR = sb("probs", [P, P_RING, 4, HALF])
        PAIR = sb("probs_pair", [P, 4, HALF])
        NOTE = sb("note", [P, 2])
        PAUSE = sb("pause", [P, 1])
        MC = sb("max_cols", [P, GROUP * QT, NH])
        NM = sb("neg_max", [P, GROUP * QT])
        NT_ = sb("neg_max_t", [GROUP * QT, P], F32R)
        AVS = sb("av_copy", [P, 2, HALF])
        RC = sb("recip", [P, HALF])
        ST = sb("stats", [P, CT, NH, 6])
        MV = sb("mean_var", [P, CT, 2])
        GM = sb("group_mean", [P, CT])
        DV = sb("deviation", [P, CT])
        SQ = sb("dev_squared", [P, CT])
        VV = sb("var_plus", [P, CT])
        VS = sb("group_var", [P, CT])
        VE = sb("var_eps", [P, CT])
        RS = sb("rstd", [P, CT])
        GA = sb("gn_scale", [P, CT])
        GB = sb("gn_shift", [P, CT])
        GT = sb("gn_shift_neg", [P, CT])

        WT = [ctx.enter_context(nc.psum_tensor(f"work{i}", [P, 2, HALF], F32)) for i in range(2)]
        AVP = ctx.enter_context(nc.psum_tensor("av", [P, HALF], F32))
        AV2 = ctx.enter_context(nc.psum_tensor("av2_or_sums", [P, HALF], F32))
        MX = [ctx.enter_context(nc.psum_tensor(f"mx{i}", [P, HALF], F32)) for i in range(2)]

        ACC = PAIR[:, 0, :]
        EDGE = SIDE + 2
        S1 = PAIR[0:3 * D, :, :].rearrange("p a b -> p (a b)")[:, 0:EDGE * EDGE].rearrange("p (r c) -> p r c", c=EDGE)
        PRF = PR[:, :, :, :].rearrange("p a b c -> p (a b c)")
        QSF = QS[:, :, :, :].rearrange("p a h n -> p (a h n)")
        S2 = PRF[0:D, 0:T]
        NR = KS[0:1, 0, :].rearrange("o (a n) -> o a n", a=2)

        NARROW_PARTS = {("q", "hi", 0): Q0[:, :], ("k", "hi", 0): K0[:, :]}
        for i, key in enumerate((("q", "lo", 0), ("k", "lo", 0), ("q", "hi", 1), ("k", "hi", 1), ("q", "lo", 1),
                                 ("k", "lo", 1))):
            NARROW_PARTS[key] = PRF[:, i * T:(i + 1) * T].bitcast(F32R)
        WIDE_PARTS = {(o, part, g): QSF[:, (4 * i + 2 * j + g) * T:(4 * i + 2 * j + g + 1) * T]
                      for i, part in enumerate(("hi", "lo")) for j, o in enumerate("qk") for g in range(2)}

        S = {n: ctx.enter_context(nc.semaphore(n)) for n in PER}
        consts = ctx.enter_context(nc.semaphore("consts"))
        folded_mm = ctx.enter_context(nc.semaphore("folded_mm"))
        folded = ctx.enter_context(nc.semaphore("folded"))
        CONSTS = 5

        def w(name, parts=P):
            a, n = AT[name]
            return W[0:parts, a:a + n]

        def wcol(name, i, parts=P, base=0):
            a, _ = AT[name]
            return W[base:base + parts, a + i:a + i + 1]

        def read(slot):
            return S[f"tile_read{slot}"]

        block = ctx.enter_context(nc.Block())

        @block.sync
        def _(sp):
            sp.dma_start(H[:, :, :], x[0].rearrange("(t p) n -> p t n", p=P)).then_inc(S["x_loaded"], 16)
            sp.dma_start(W[:, :], pack).then_inc(S["x_res_free"], 16)
            sp.dma_start(E[:, :, :], pos.rearrange("(t p) n -> p t n", p=P)).then_inc(S["pos_loaded"], 16)
            with sp.Fori(0, SAMPLES) as b:
                c = Count(b)

                def stacks(att):
                    tiles = [c.tile() for _ in range(6)]
                    if att.wide:
                        return
                    for g in range(2):
                        sp.wait_ge(read(tiles[2 * g] % 2), c.tile_read(tiles[2 * g]))
                        sp.wait_ge(read(tiles[2 * g + 1] % 2), c.tile_read(tiles[2 * g + 1]))
                        done = S[f"stack_ready{g}"]
                        for j in range(GROUP):
                            h, rows = GROUP * g + j, slice(D * j, D * j + D)
                            q_hi, q_lo, k_hi, k_lo = (NARROW_PARTS[o, part, g][rows, :].bitcast(F32)
                                                      for o in "qk" for part in ("hi", "lo"))
                            for i, part in enumerate((q_hi, q_lo, q_hi)):
                                sp.dma_start(QS[D * i:D * i + D, :, h, :].bitcast(F32),
                                             part.rearrange("p (a n) -> p a n", a=NH)).then_inc(done, 16)
                            for i, part in enumerate((k_hi, k_hi, k_lo)):
                                sp.dma_start(KS[D * i:D * i + D, h, :].bitcast(F32), part).then_inc(done, 16)

                def rows(att):
                    for u, qh in att.steps:
                        n = c.mx(att.maxima + 1)
                        sp.wait_ge(S["mx_read"], c.at("mx_read", n + 1))
                        sp.dma_start(QS[96:97, qh, GROUP * u:GROUP * u + GROUP, :]
                                     .rearrange("o h (a n) -> o (h a) n", n=P).bitcast(F32),
                                     NT_[:, :].bitcast(F32)).then_inc(S["row_ready"], 16)
                        for _ in range(att.items * att.tiles):
                            c.tile()

                def wide_rows(att):
                    steps = len(att.steps)
                    for s in range(steps):
                        if s >= 2:
                            c.mx(1)
                        n = c.mx(att.maxima + 1)
                        sp.wait_ge(S["mx_read"], c.at("mx_read", n + 1))
                        sp.dma_start(NR[0:1, s % 2, :].rearrange("o (a n) -> o a n", n=P).bitcast(F32),
                                     NT_[0:QT, :].bitcast(F32)).then_inc(S["row_ready"], 16)
                        for _ in range(att.items * att.tiles):
                            c.tile()
                    c.mx(min(2, steps))

                c.mx(2)
                stacks(ATT0)
                rows(ATT0)
                for _ in range(NH + 4):
                    c.tile()
                c.mx(4)
                stacks(ATT1)
                rows(ATT1)
                stacks(ATTM)
                wide_rows(ATTM)
                for _ in range(3 * NH):
                    n = c.tile()
                sp.wait_ge(read(n % 2), c.tile_read(n))
                sp.dma_start(H[:, :, :], x[(b + 1) % SAMPLES].rearrange("(t p) n -> p t n", p=P))\
                  .then_inc(S["x_loaded"], 16)
                sp.dma_start(E[:, :, :], pos.rearrange("(t p) n -> p t n", p=P)).then_inc(S["pos_loaded"], 16)
                c.mx(4)
                stacks(ATT2)
                rows(ATT2)
                for _ in range(NH):
                    c.tile()
                c.mx(2)
                stacks(ATT3)
                wide_rows(ATT3)
                for _ in range(NH):
                    n = c.tile()
                    sp.wait_ge(read(n % 2), c.tile_read(n))
                sp.dma_start(out[b].rearrange("(t p) n -> p t n", p=P), X[:, :, :]).then_inc(S["x_res_free"], 16)
            sp.wait_ge(S["x_res_free"], 16 * (SAMPLES + 1))
            sp.wait_ge(S["x_loaded"], 16 * (SAMPLES + 1))
            sp.wait_ge(S["pos_loaded"], 16 * (SAMPLES + 1))

        @block.gpsimd
        def _(pool):
            pool.memset(ONES[:, :], 1.0).then_inc(consts, 1)
            pool.memset(POWER[:, :], -0.5).then_inc(consts, 1)
            for i, ones in enumerate((ONEROW[:, :], KS[96:97, 0:GROUP, :], KS[96:97, GROUP:, :])):
                pool.wait_ge(consts, 2 + i)
                pool.memset(ones.bitcast(F32), 1.0).then_inc(consts, 1)
            pool.wait_ge(consts, CONSTS)
            with pool.Fori(0, SAMPLES) as b:
                c = Count(b)

                def rstd():
                    pool.wait_ge(S["gn_var"], c.next("gn_var"))
                    pool.tensor_tensor(RS[:, :], VE[:, :], POWER[:, :], ALU.pow).then_inc(S["gn_rstd"], 1)

                def pairs(att):
                    for _ in range(6):
                        c.tile()
                    for s in range(len(att.steps)):
                        for i in range(att.items):
                            made = [c.tile() for _ in range(att.tiles)]
                            m = slot[0]
                            slot[0] += 1
                            if i % 2 == 1 and i < 2 * att.pairs(s):
                                for n in made:
                                    pool.wait_ge(read(n % 2), c.tile_read(n))
                                if pair[0]:
                                    pool.wait_ge(S["pair_used"], c.at("pair_used", pair[0]))
                                pair[0] += 1
                                pool.tensor_tensor(PAIR[:, :, :].rearrange("p a b -> p (a b)"),
                                                   PR[:, (m - 1) % P_RING, :, :].rearrange("p a b -> p (a b)"),
                                                   PR[:, m % P_RING, :, :].rearrange("p a b -> p (a b)"), ALU.add)\
                                    .then_inc(S["pair_ready"], 1)

                def skip(att):
                    for _ in range(6 + len(att.steps) * att.items * att.tiles):
                        c.tile()
                    slot[0] += len(att.steps) * att.slots

                slot, pair = [0], [0]
                rstd()
                pairs(ATT0)
                rstd()
                rstd()
                for _ in range(NH + 4):
                    c.tile()
                pairs(ATT1)
                skip(ATTM)
                for _ in range(3 * NH):
                    c.tile()
                rstd()
                rstd()
                pairs(ATT2)
                rstd()

        @block.scalar
        def _(act):
            act.wait_ge(S["x_res_free"], 16)
            act.wait_ge(consts, CONSTS)
            with act.Fori(0, SAMPLES) as b:
                c = Count(b)
                slot = [0]
                steps = [0]
                summed = [0]

                def qkv(att):
                    for i in range(6):
                        n = c.tile()
                        act.wait_ge(S["tile_full"], c.tile_full(n))
                        src = WT[n % 2][:, :, :].rearrange("p a b -> p (a b)")
                        if i < 4:
                            g, o = i // 2, "qk"[i % 2]
                            dst = (WIDE_PARTS if att.wide else NARROW_PARTS)[o, "hi", g]
                            if att.biased:
                                ins = act.activation(dst, src, ACT.Identity, bias=wcol(f"b{o}{att.name}", g))
                            else:
                                ins = act.activation(dst, src, ACT.Identity)
                            ins.then_inc(S["hi_ready"], 1)
                        else:
                            k = 4 * (i - 4)
                            act.activation(VT[:, k:k + 4, :].rearrange("p a b -> p (a b)"), src, ACT.Identity)\
                               .then_inc(read(n % 2), 1)
                def evacuate(att):
                    act.wait_ge(S["p_used"], c.at("p_used", slot_end[0]))
                    if steps[0]:
                        act.wait_ge(S["av_normed"], c.at("av_normed", steps[0]))
                    second = AV2 if (not att.wide or att.ctiles == 2) else None
                    if second is None:
                        act.activation(AVS[:, 0, :], AVP[:, :], ACT.Identity).then_inc(S["av_read"], 1)
                    else:
                        act.activation(AVS[:, 0, :], AVP[:, :], ACT.Identity)
                        act.activation(AVS[:, 1, :], second[:, :], ACT.Identity).then_inc(S["av_read"], 1)
                    steps[0] += 1

                slot_end = [0]

                def attention(att):
                    first_slot, first_sum = slot[0], summed[0]
                    for s in range(len(att.steps)):
                        for i in range(att.items):
                            for t in range(att.tiles):
                                half = i % 2 if att.wide else t
                                if half == 0 and slot[0] >= P_RING:
                                    act.wait_ge(S["p_used"], c.at("p_used", slot[0] - P_RING + 1))
                                    if att.wide and slot[0] - first_slot >= P_RING:
                                        act.wait_ge(S["p_summed"], c.at("p_summed", summed[0] - P_RING + 1))
                                if half == 0 and not att.wide:
                                    if s == 0 and i == 1:
                                        act.wait_ge(S["stack_ready1"], c.next("stack_ready1", 16 * 24))
                                    if i % 2 == 1 and 0 < i // 2 <= att.pairs(s):
                                        act.wait_ge(S["pair_ready"], c.next("pair_ready"))
                                n = c.tile()
                                act.wait_ge(S["tile_full"], c.tile_full(n))
                                act.activation(PR[:, slot[0] % P_RING, 2 * half:2 * half + 2, :], WT[n % 2][:, :, :],
                                               ACT.Exp, scale=att.scale).then_inc(read(n % 2), 1)
                                if half == 1:
                                    slot[0] += 1
                                    if att.wide:
                                        summed[0] += 1
                            if i == 0 and s > 0:
                                evacuate(att)
                        slot_end[0] = slot[0]
                    evacuate(att)

                for att in LAYERS:
                    qkv(att)
                    attention(att)
                    if att in (ATT0, ATT2, ATT3):
                        for _ in range(NH):
                            c.tile()
                    if att is ATT0:
                        act.wait_ge(S["border"], c.next("border"))
                        n = c.tile()
                        act.wait_ge(S["tile_full"], c.tile_full(n))
                        for j in range(3):
                            ins = act.activation(
                                S1[D * j:D * j + D, 1:SIDE + 1, 2 - j:2 - j + SIDE],
                                WT[n % 2][D * j:D * j + D, :, :].rearrange("p a (r c) -> p (a r) c", c=SIDE),
                                ACT.Silu, bias=wcol("bsa1", 0, D, D * j))
                        ins.then_inc(read(n % 2), 1)
                        n = c.tile()
                        act.wait_ge(S["tile_full"], c.tile_full(n))
                        act.activation(S2[:, :], WT[n % 2][0:D, :, :].rearrange("p a b -> p (a b)"), ACT.Silu,
                                       bias=wcol("bsa2", 0, D)).then_inc(read(n % 2), 1)
                        for nh in range(NH):
                            n = c.tile()
                            act.wait_ge(S["tile_full"], c.tile_full(n))
                            act.activation(AO[:, 0, nh * HALF:(nh + 1) * HALF], WT[n % 2][:, 0, :], ACT.Sigmoid,
                                           bias=wcol("bsa3", 0)).then_inc(read(n % 2), 1)
                    if att is ATTM:
                        for dst, bias, func in ((H, "bff1", ACT.Silu), (E, "bff2", ACT.Identity),
                                                (A, "bffo", ACT.Identity)):
                            for nh in range(NH):
                                n = c.tile()
                                act.wait_ge(S["tile_full"], c.tile_full(n))
                                for m in range(CT):
                                    ins = act.activation(dst[:, m, nh * HALF:(nh + 1) * HALF], WT[n % 2][:, m, :],
                                                         func, bias=wcol(bias, m))
                                ins.then_inc(read(n % 2), 1)

        @block.vector
        def _(dve):
            dve.wait_ge(S["x_res_free"], 16)
            dve.wait_ge(folded_mm, 1)
            for i, l in enumerate("023"):
                ins = dve.tensor_tensor(BOUT[:, i, :], MX[0][:, CT * i:CT * i + CT], w(f"bp{l}"), ALU.add)
            ins.then_inc(folded, 1)
            dve.wait_ge(folded, 1)
            total = {}
            with dve.Fori(0, SAMPLES) as b:
                c = Count(b)

                def chain(ins):
                    ins.then_inc(S["vec"], 1)
                    dve.wait_ge(S["vec"], c.next("vec"))

                def norm(src, name, eps, apply):
                    for t in range(CT):
                        for nh in range(NH):
                            ins = dve.bn_stats(ST[:, t, nh, :], src[:, t, nh * HALF:(nh + 1) * HALF])
                    chain(ins)
                    dve.memset(PAUSE[:, :], 0.0)
                    for t in range(CT):
                        ins = dve.bn_aggr(MV[:, t, :], ST[:, t, :, :].rearrange("p a b -> p (a b)"))
                    ins.then_inc(S["gn_mean"], 1)
                    dve.wait_ge(S["gn_mean"], c.next("gn_mean"))
                    n = c.mx()
                    dve.wait_ge(S["mx_full"], c.at("mx_full", n + 1))
                    dve.tensor_copy(GM[:, :], MX[n % 2][:, 0:CT]).then_inc(S["mx_read"], 1)
                    dve.wait_ge(S["mx_read"], c.at("mx_read", n + 1))
                    chain(dve.tensor_tensor(DV[:, :], MV[:, :, 0], GM[:, :], ALU.subtract))
                    chain(dve.tensor_tensor(SQ[:, :], DV[:, :], DV[:, :], ALU.mult))
                    dve.tensor_tensor(VV[:, :], SQ[:, :], MV[:, :, 1], ALU.add).then_inc(S["gn_dev"], 1)
                    n = c.mx()
                    dve.wait_ge(S["mx_full"], c.at("mx_full", n + 1))
                    dve.tensor_copy(VS[:, :], MX[n % 2][:, 0:CT]).then_inc(S["mx_read"], 1)
                    dve.wait_ge(S["mx_read"], c.at("mx_read", n + 1))
                    dve.tensor_scalar(VE[:, :], VS[:, :], eps, None, ALU.add).then_inc(S["gn_var"], 1)
                    dve.wait_ge(S["gn_rstd"], c.next("gn_rstd"))
                    chain(dve.tensor_tensor(GA[:, :], RS[:, :], w(f"gw{name}"), ALU.mult))
                    chain(dve.tensor_tensor(GT[:, :], GM[:, :], GA[:, :], ALU.mult))
                    chain(dve.tensor_tensor(GB[:, :], w(f"gb{name}"), GT[:, :], ALU.subtract))
                    for t in range(CT):
                        apply(t, GA[:, t:t + 1], GB[:, t:t + 1])

                def apply_to(src, dst):
                    def apply(t, scale, shift):
                        dve.tensor_scalar(dst[:, t, :], src[:, t, :], scale, shift, ALU.mult, ALU.add)\
                           .then_inc(S["act_ready"], 1)
                        c.next("act_ready")
                    return apply

                def maxima(att, k):
                    for _ in range(k):
                        n = c.mx()
                        i = mi[0]
                        mi[0] += 1
                        dve.wait_ge(S["mx_full"], c.at("mx_full", n + 1))
                        if att.wide:
                            col, kh = i // NH, i % NH
                        else:
                            qt, kh, j = i // (NH * GROUP), i // GROUP % NH, i % GROUP
                            col = j * QT + qt
                        dve.tensor_reduce(MC[:, col, kh:kh + 1], MX[n % 2][:, :], AX.X, ALU.max)\
                           .then_inc(S["mx_read"], 1)
                    if mi[0] == att.maxima and k:
                        cols = QT if att.wide else GROUP * QT
                        dve.wait_ge(S["mx_read"], c.at("mx_read", n + 1))
                        dve.tensor_reduce(NM[:, 0:cols], MC[:, 0:cols, :], AX.X, ALU.max, negate=True)\
                           .then_inc(S["nm_ready"], 1)
                        c.next("nm_ready")

                mi = [0]

                def columns(att):
                    cols = QT if att.wide else GROUP * QT
                    n = c.mx()
                    if c.n.get("row_ready"):
                        dve.wait_ge(S["row_ready"], c.at("row_ready", c.n["row_ready"]))
                    dve.wait_ge(S["mx_full"], c.at("mx_full", n + 1))
                    dve.tensor_copy(NT_[0:cols, :], MX[n % 2][0:cols, 0:P]).then_inc(S["mx_read"], 1)
                    c.next("row_ready", 16)
                    mi[0] = 0

                def qkv(att):
                    parts = WIDE_PARTS if att.wide else NARROW_PARTS
                    for i in range(6):
                        n = c.tile()
                        maxima(att, att.lead[i])
                        if i < 4:
                            g, o = i // 2, "qk"[i % 2]
                            dve.wait_ge(S["hi_ready"], c.next("hi_ready"))
                            dve.scalar_tensor_tensor(
                                out=parts[o, "lo", g], in0=WT[n % 2][:, :, :].rearrange("p a b -> p (a b)"),
                                scalar=wcol(f"b{o}{att.name}", g) if att.biased else 0.0,
                                in1=parts[o, "hi", g].bitcast(F32), op0=ALU.add, op1=ALU.subtract)\
                                .then_inc(read(n % 2), 1)
                    columns(att)

                def normalize(att, s, dst):
                    u, qh = att.steps[s]
                    cols = slice(qh * HALF, (qh + 1) * HALF)
                    if att.wide:
                        n = c.mx()
                        dve.wait_ge(S["mx_full"], c.at("mx_full", n + 1))
                        dve.reciprocal(RC[:, :], MX[n % 2][:, :]).then_inc(S["mx_read"], 1)
                        dve.wait_ge(S["mx_read"], c.at("mx_read", n + 1))
                        dve.wait_ge(S["av_read"], c.next("av_read"))
                    else:
                        dve.wait_ge(S["av_read"], c.next("av_read"))
                        chain(dve.reciprocal(RC[:, :], AVS[:, 1, :]))
                    for d in range(att.ctiles):
                        ins = dve.tensor_tensor(dst[:, u + d, cols], AVS[:, d, :], RC[:, :], ALU.mult)
                    ins.then_inc(S["av_normed"], 1)

                def accumulate(att, i):
                    n = c.tile()
                    dve.wait_ge(read(n % 2), c.tile_read(n))
                    half, m = i % 2, wide_slot[0]
                    for jj in range(2):
                        pt = PR[:, slot_at(m), 2 * half + jj, :]
                        if i == 0 and jj == 0:
                            continue
                        prev = PR[:, slot_at(m), 0, :] if i == 0 else ACC
                        ins = dve.tensor_tensor(ACC, prev, pt, ALU.add)
                        if i == att.items - 1 and jj == 1:
                            chain(ins)
                            dve.tensor_copy(NOTE[:, 0:1], PAIR[:, 0, 0:1]).then_inc(S["acc_ready"], 1)
                            dve.tensor_copy(NOTE[:, 1:2], PAIR[:, 0, 0:1]).then_inc(S["p_summed"], 1)
                        elif half == 1 and jj == 1:
                            ins.then_inc(S["p_summed"], 1)
                            dve.wait_ge(S["p_summed"], c.at("p_summed", c.n.get("p_summed", 0) + 1))
                        else:
                            chain(ins)
                    if half == 1:
                        c.next("p_summed")
                        wide_slot[0] += 1

                wide_slot = [0]

                def slot_at(m):
                    return (m + slots_before[0]) % P_RING

                slots_before = [0]

                def attention(att, dst):
                    wide_slot[0] = 0
                    steps = len(att.steps)
                    slots_before[0] = sum(len(a.steps) * a.slots for a in LAYERS[:LAYERS.index(att)])
                    for s in range(steps):
                        for i in range(att.items):
                            if s + 1 < steps:
                                maxima(att, att.spread[i])
                                if i == att.items - 1:
                                    columns(att)
                            if s > 0 and i == (0 if att.wide else att.items - 1 if s + 1 < steps else 0):
                                normalize(att, s - 1, dst)
                            if att.wide:
                                accumulate(att, i)
                            else:
                                c.tile()
                                c.tile()
                    normalize(att, steps - 1, dst)

                def project(i, residual):
                    for nh in range(NH):
                        n = c.tile()
                        dve.wait_ge(S["tile_full"], c.tile_full(n))
                        for m in range(CT):
                            cols = slice(nh * HALF, (nh + 1) * HALF)
                            ins = dve.scalar_tensor_tensor(out=X[:, m, cols], in0=WT[n % 2][:, m, :],
                                                           scalar=BOUT[:, i, m:m + 1], in1=residual[:, m, cols],
                                                           op0=ALU.add, op1=ALU.add)
                        ins.then_inc(read(n % 2), 1)
                    dve.wait_ge(read(n % 2), c.tile_read(n))

                dve.wait_ge(S["x_loaded"], c.next("x_loaded", 16))
                norm(H, "0", 1e-5, apply_to(H, A))
                qkv(ATT0)
                attention(ATT0, AO)
                dve.memset(S1, 0.0).then_inc(S["border"], 1)
                dve.wait_ge(S["x_res_free"], c.next("x_res_free", 16))
                project(0, H)

                def apply_pre(t, scale, shift):
                    chain(dve.tensor_scalar(A[:, t, :], X[:, t, :], scale, shift, ALU.mult, ALU.add))
                    dve.tensor_tensor(A[:, t, :], A[:, t, :], E[:, t, :], ALU.add).then_inc(S["act_ready"], 1)
                    c.next("act_ready")
                    dve.wait_ge(S["act_ready"], c.at("act_ready", c.n["act_ready"]))

                dve.wait_ge(S["pos_loaded"], c.next("pos_loaded", 16))
                norm(X, "pre", 1e-6, apply_pre)
                norm(A, "norm", 1e-6, apply_to(A, H))
                for _ in range(2):
                    c.tile()
                for nh in range(NH):
                    n = c.tile()
                    dve.wait_ge(read(n % 2), c.tile_read(n))
                for t in range(CT):
                    dve.tensor_tensor(E[:, t, :], A[:, t, :], AO[:, 0, :], ALU.mult).then_inc(S["act_ready"], 1)
                    c.next("act_ready")
                dve.wait_ge(S["act_ready"], c.at("act_ready", c.n["act_ready"]))
                qkv(ATT1)
                attention(ATT1, AO)
                qkv(ATTM)
                attention(ATTM, A)
                for _ in range(2 * NH):
                    c.tile()
                for nh in range(NH):
                    n = c.tile()
                    dve.wait_ge(read(n % 2), c.tile_read(n))

                def apply_post(t, scale, shift):
                    chain(dve.scalar_tensor_tensor(out=X[:, t, :], in0=A[:, t, :], scalar=scale, in1=X[:, t, :],
                                                   op0=ALU.mult, op1=ALU.add))
                    chain(dve.tensor_scalar(X[:, t, :], X[:, t, :], shift, None, ALU.add))

                norm(A, "post", 1e-6, apply_post)

                norm(X, "2", 1e-5, apply_to(X, A))
                qkv(ATT2)
                attention(ATT2, AO)
                project(1, A)

                norm(X, "3", 1e-5, apply_to(X, A))
                qkv(ATT3)
                attention(ATT3, AO)
                project(2, X)
                total.update(c.n)
            assert total["vec"] == PER["vec"], f"vec {total['vec']}"
            assert total["act_ready"] == PER["act_ready"], total
            assert total["tile"] + 1 == N_TILES and total["mx"] + 1 == N_MX, (total, N_TILES, N_MX)

        @block.tensor
        def _(pe):
            def mm(dst, lhsT, rhs, start, stop, **kw):
                return nc.tensor.matmul(dst, lhsT, rhs, start=start, stop=stop, **kw)

            pe.wait_ge(S["x_res_free"], 16)
            pe.wait_ge(consts, CONSTS)
            for i, l in enumerate("023"):
                wp = w(f"wp{l}").rearrange("p (k n) -> p k n", k=CT)
                for m in range(CT):
                    for k in range(CT):
                        ins = mm(MX[0][:, CT * i + m:CT * i + m + 1], wp[:, k, m * P:(m + 1) * P],
                                 wcol(f"bv{l}", k), k == 0, k == CT - 1)
            ins.then_inc(folded_mm, 1)
            pe.wait_ge(folded, 1)
            total = {}
            with pe.Fori(0, SAMPLES) as b:
                c = Count(b)

                def new_tile():
                    n = c.tile()
                    if n >= 2:
                        pe.wait_ge(read(n % 2), c.tile_free(n))
                    return n, WT[n % 2]

                def new_bank():
                    n = c.mx()
                    if n >= 2:
                        pe.wait_ge(S["mx_read"], c.at("mx_read", n - 1))
                    return MX[n % 2]

                def group_means():
                    bank = new_bank()
                    pe.wait_ge(S["gn_mean"], c.next("gn_mean"))
                    mm(bank[:, 0:CT], w("gmean"), MV[:, :, 0], True, True).then_inc(S["mx_full"], 1)
                    bank = new_bank()
                    pe.wait_ge(S["gn_dev"], c.next("gn_dev"))
                    mm(bank[:, 0:CT], w("gmean"), VV[:, :], True, True).then_inc(S["mx_full"], 1)

                mi = [0]

                def maxima(att, s, k):
                    for _ in range(k):
                        u, qh = att.steps[s]
                        i = mi[0]
                        mi[0] += 1
                        bank = new_bank()
                        if att.wide:
                            qt, kh = i // NH, i % NH
                            q0 = qh * HALF + qt * P
                            for ct in range(att.ctiles):
                                ins = mm(bank[:, :], WIDE_PARTS["q", "hi", u + ct][:, q0:q0 + P],
                                         WIDE_PARTS["k", "hi", u + ct][:, kh * HALF:(kh + 1) * HALF],
                                         ct == 0, ct == att.ctiles - 1)
                        else:
                            qt, kh, j = i // (NH * GROUP), i // GROUP % NH, i % GROUP
                            q0 = qh * HALF + qt * P
                            if s == 0:
                                r = slice(D * j, D * j + D)
                                ins = mm(bank[:, :], Q0[r, q0:q0 + P], K0[r, kh * HALF:(kh + 1) * HALF], True, True,
                                         tile_position=(D * j, 0))
                            else:
                                h = GROUP * u + j
                                ins = mm(bank[:, :], QS[0:96, qh, h, qt * P:(qt + 1) * P],
                                         KS[0:96, h, kh * HALF:(kh + 1) * HALF], True, True)
                        ins.then_inc(S["mx_full"], 1)

                def columns(att):
                    cols = QT if att.wide else GROUP * QT
                    bank = new_bank()
                    pe.wait_ge(S["nm_ready"], c.next("nm_ready"))
                    nc.tensor.transpose(bank[0:cols, 0:P], NM[:, 0:cols], w("ident")).then_inc(S["mx_full"], 1)
                    mi[0] = 0

                def qkv(att, src_q, src_kv, wq, wk, wv):
                    tiles = []
                    for i in range(6):
                        n, tile = new_tile()
                        tiles.append(n)
                        if att.lead[i] and mi[0] == 0:
                            for t in tiles[2:4] if att.ctiles == 2 else tiles[:2]:
                                pe.wait_ge(read(t % 2), c.tile_read(t))
                        left = [att.lead[i]]

                        def between(k):
                            k = min(k, left[0])
                            left[0] -= k
                            maxima(att, 0, k)

                        if i < 4:
                            g, src, wt = i // 2, (src_q, src_kv)[i % 2], w((wq, wk)[i % 2])
                            wt = wt.rearrange("p (g k n) -> p g k n", g=2, k=CT)
                            for nh in range(NH):
                                for k in range(CT):
                                    between(2)
                                    ins = mm(tile[:, nh, :], wt[:, g, k, :], src[:, k, nh * HALF:(nh + 1) * HALF],
                                             k == 0, k == CT - 1)
                        else:
                            wt = w(wv).rearrange("p (k n) -> p k n", k=CT)
                            for t in range(4):
                                tok = (4 * (i - 4) + t) * P
                                for k in range(CT):
                                    between(1)
                                    ins = mm(tile[:, t // 2, t % 2 * C:(t % 2 + 1) * C], src_kv[:, k, tok:tok + P],
                                             wt[:, k, :], k == 0, k == CT - 1)
                        ins.then_inc(S["tile_full"], 1)
                        between(left[0])
                    columns(att)
                    for t in tiles[4:]:
                        pe.wait_ge(read(t % 2), c.tile_read(t))
                    if not att.wide:
                        pe.wait_ge(S["stack_ready0"], c.next("stack_ready0", 16 * 24))

                def scores(att, s, i, between):
                    u, qh = att.steps[s]
                    qs = slice(qh * HALF, (qh + 1) * HALF)
                    made = []
                    for t in range(att.tiles):
                        n, tile = new_tile()
                        made.append(n)
                        for jj in range(2):
                            if att.wide:
                                ks = slice((2 * i + jj) * P, (2 * i + jj + 1) * P)
                                for ct in range(att.ctiles):
                                    k_hi, k_lo, q_hi, q_lo = (WIDE_PARTS[o, part, u + ct][:, x] for o, x in
                                                              (("k", ks), ("q", qs)) for part in ("hi", "lo"))
                                    mm(tile[:, jj, :], k_hi, q_hi, ct == 0, False)
                                    mm(tile[:, jj, :], k_hi, q_lo, False, False)
                                    mm(tile[:, jj, :], k_lo, q_hi, False, False)
                                ins = mm(tile[:, jj, :], ONEROW[:, :], NR[0:1, s % 2, :], False, True)
                                if jj == 0:
                                    between()
                            else:
                                h = GROUP * u + 2 * t + jj
                                ins = mm(tile[:, jj, :], KS[0:97, h, i * P:(i + 1) * P], QS[0:97, qh, h, :],
                                         True, True)
                        ins.then_inc(S["tile_full"], 1)
                        between()
                    return made

                slot = [0]
                step = [0]

                def values(att, s, i, made, between):
                    u, _ = att.steps[s]
                    for n in made:
                        pe.wait_ge(read(n % 2), c.tile_read(n))
                    if i == 0:
                        if step[0]:
                            pe.wait_ge(S["av_read"], c.at("av_read", step[0]))
                        step[0] += 1
                    pt = PR[:, slot[0] % P_RING, :, :]
                    if att.wide:
                        for jj in range(2):
                            kt = 2 * i + jj
                            for d in range(att.ctiles):
                                col = (u + d) * P
                                ins = mm((AVP, AV2)[d][:, :], VT[:, kt, col:col + P], pt[:, 2 * (i % 2) + jj, :],
                                         kt == 0, kt == KT - 1)
                            if jj == 1 and i % 2 == 1:
                                ins.then_inc(S["p_used"], 1)
                                slot[0] += 1
                            between()
                        if i == att.items - 1:
                            bank = new_bank()
                            pe.wait_ge(S["acc_ready"], c.next("acc_ready"))
                            mm(bank[:, :], ONES[:, :], ACC, True, True).then_inc(S["mx_full"], 1)
                        return

                    def sums(p, start, stop):
                        for j in range(GROUP):
                            ins = mm(AV2[D * j:D * j + D, :], ONES[:, 0:D], p[:, j, :], start, stop,
                                     tile_position=(0, D * j))
                        return ins

                    for j in range(GROUP):
                        h = GROUP * u + j
                        ins = mm(AVP[D * j:D * j + D, :], VT[:, i, D * h:D * h + D], pt[:, j, :], i == 0,
                                 i == KT - 1, tile_position=(0, D * j))
                    paired = 2 * att.pairs(s)
                    if i < paired:
                        ins.then_inc(S["p_used"], 1)
                    between()
                    if i % 2 == 0 and 0 < i <= paired:
                        pe.wait_ge(S["pair_ready"], c.next("pair_ready"))
                        sums(PAIR, i == 2, False).then_inc(S["pair_used"], 1)
                    between()
                    if i >= paired:
                        sums(pt, i == 0, i == KT - 1).then_inc(S["p_used"], 1)
                    slot[0] += 1

                def attention(att):
                    behind = None
                    for s in range(len(att.steps)):
                        for i in range(att.items):
                            more = s + 1 < len(att.steps)
                            if i == 0:
                                pe.wait_ge(S["row_ready"], c.next("row_ready", 16))
                                if s == 1 and not att.wide:
                                    pe.wait_ge(S["stack_ready1"], c.next("stack_ready1", 16 * 24))
                            if more and i == att.items - 1:
                                columns(att)
                            left = [att.spread[i] if more else 0]

                            def between():
                                if left[0]:
                                    left[0] -= 1
                                    maxima(att, s + 1, 1)

                            made = scores(att, s, i, between)
                            if behind is not None:
                                if att.wide and i == 0:
                                    maxima(att, s + 1, left[0])
                                    left[0] = 0
                                values(att, *behind, between)
                            if left[0]:
                                maxima(att, s + 1, left[0])
                            behind = (s, i, made)
                    values(att, *behind, lambda: None)

                def dense(srcs, weights, ready):
                    wt = w(weights).rearrange("p (k n) -> p k n", n=C)
                    made = []
                    for nh in range(NH):
                        n, tile = new_tile()
                        ready(nh)
                        made.append(n)
                        for m in range(CT):
                            for k in range(CT * len(srcs)):
                                ins = mm(tile[:, m, :], wt[:, k, m * P:(m + 1) * P],
                                         srcs[k // CT][:, k % CT, nh * HALF:(nh + 1) * HALF],
                                         k == 0, k == CT * len(srcs) - 1)
                        ins.then_inc(S["tile_full"], 1)
                    return made

                def normed(half_steps):
                    def ready(nh):
                        pe.wait_ge(S["av_normed"], c.at("av_normed", step[0] - (0 if nh else half_steps)))
                    return ready

                def wait_tiles(made):
                    def ready(nh):
                        pe.wait_ge(read(made[nh] % 2), c.tile_read(made[nh]))
                    return ready

                group_means()
                pe.wait_ge(S["act_ready"], c.next("act_ready", 2))
                qkv(ATT0, A, A, "wq0", "wk0", "wv0")
                attention(ATT0)
                dense([AO], "wp0", normed(2))

                group_means()
                n, tile = new_tile()
                pe.wait_ge(S["act_ready"], c.next("act_ready", 2))
                w1 = w("sa1").rearrange("p (k n) -> p k n", k=CT)
                for nh in range(NH):
                    for k in range(CT):
                        ins = mm(tile[0:3 * D, nh, :], w1[:, k, :], A[:, k, nh * HALF:(nh + 1) * HALF],
                                 k == 0, k == CT - 1)
                ins.then_inc(S["tile_full"], 1)
                group_means()
                pe.wait_ge(read(n % 2), c.tile_read(n))
                n, tile = new_tile()
                w2 = w("sa2", 3 * D).rearrange("p (k n) -> p k n", k=3)
                rows = SIDE // NH
                for nh in range(NH):
                    for dy in range(3):
                        ins = mm(tile[0:D, nh, :], w2[:, dy, :],
                                 S1[:, dy + rows * nh:dy + rows * (nh + 1), 1:SIDE + 1], dy == 0, dy == 2)
                ins.then_inc(S["tile_full"], 1)
                pe.wait_ge(read(n % 2), c.tile_read(n))
                for nh in range(NH):
                    n, tile = new_tile()
                    mm(tile[:, 0, :], w("sa3", D), S2[:, nh * HALF:(nh + 1) * HALF], True, True)\
                        .then_inc(S["tile_full"], 1)
                pe.wait_ge(S["act_ready"], c.next("act_ready", 2))
                qkv(ATT1, H, H, "wq1", "wk1", "wv1")
                attention(ATT1)
                pe.wait_ge(S["act_ready"], c.next("act_ready", 2))
                qkv(ATTM, E, H, "mq", "mk", "mv")
                attention(ATTM)
                made = dense([AO, A], "ff1", normed(1))
                made = dense([H], "ff2", wait_tiles(made))
                dense([E], "ffo", wait_tiles(made))
                group_means()

                group_means()
                pe.wait_ge(S["act_ready"], c.next("act_ready", 2))
                qkv(ATT2, A, A, "wq2", "wk2", "wv2")
                attention(ATT2)
                dense([AO], "wp2", normed(2))

                group_means()
                pe.wait_ge(S["act_ready"], c.next("act_ready", 2))
                qkv(ATT3, A, A, "wq3", "wk3", "wv3")
                attention(ATT3)
                dense([AO], "wp3", normed(1))
                total.update(c.n)
            assert total["tile"] + 1 == N_TILES and total["mx"] + 1 == N_MX, (total, N_TILES, N_MX)


def lay_out(a):
    f = np.float32

    def rows(m, order):
        return np.asarray(m)[order]

    def stationary(m):
        return np.asarray(m).reshape(2, P, CT, P).transpose(3, 0, 2, 1).reshape(P, -1)

    def moving(m):
        m = np.asarray(m)
        return m.reshape(m.shape[0], -1, P).transpose(2, 1, 0).reshape(P, -1)

    def cols(v):
        return np.asarray(v).reshape(CT, P).T

    def padded(m):
        m = np.asarray(m)
        return np.concatenate([m, np.zeros((P - m.shape[0], m.shape[1]), f)])

    heads = np.arange(3 * C).reshape(C // D, 3, D)
    split = [heads[:, i].reshape(-1) for i in range(3)]
    plain = [np.arange(C) + i * C for i in range(3)]
    v = {}
    for l, order, proj in (("0", split, "proj"), ("2", split, "proj"), ("3", plain, "out")):
        wt, bs = a[f"L{l}_conv_qkv_w"], a[f"L{l}_conv_qkv_b"]
        v[f"wq{l}"], v[f"wk{l}"] = (stationary(rows(wt, order[i])) for i in range(2))
        v[f"wv{l}"] = moving(rows(wt, order[2]))
        v[f"wp{l}"] = moving(a[f"L{l}_conv_{proj}_w"])
        for i, n in enumerate(("bq", "bk", "bv")):
            v[f"{n}{l}"] = cols(rows(bs, order[i]))
        v[f"bp{l}"] = cols(a[f"L{l}_conv_{proj}_b"])
        v[f"gw{l}"], v[f"gb{l}"] = cols(a[f"L{l}_conv_gn_w"]), cols(a[f"L{l}_conv_gn_b"])
    one = {k[8:]: np.asarray(x) for k, x in a.items() if k.startswith("L1_conv_")}
    v["wq1"], v["wk1"], v["wv1"] = stationary(one["wq"]), stationary(one["wk"]), moving(one["wv"])
    v["mq"] = stationary(np.concatenate([one["wq0"], one["wq1"]]))
    v["mk"] = stationary(np.concatenate([one["wk0"], one["wk1"]]))
    v["mv"] = moving(np.concatenate([one["wv0"], one["wv1"]]))
    v["ff1"], v["ff2"], v["ffo"] = moving(one["ff_w1"]), moving(one["ff_w2"]), moving(one["out_w"])
    v["sa1"] = moving(np.tile(one["sa_w1"].reshape(D, C), (3, 1)))
    v["sa2"] = padded(one["sa_w2"].transpose(3, 1, 2, 0).reshape(3 * D, 3 * D))
    v["sa3"] = padded(np.tile(one["sa_w3"].reshape(1, D), (P, 1)).T)
    v["ident"] = np.eye(P, dtype=f)
    v["gmean"] = np.kron(np.eye(P // 8, dtype=f), np.full((8, 8), 1 / 8, f))
    for n in ("pre", "norm", "post"):
        v[f"gw{n}"], v[f"gb{n}"] = cols(one[f"{n}_g"]), cols(one[f"{n}_b"])
    v["bsa1"] = padded(np.tile(one["sa_b1"], 3)[:, None])
    v["bsa2"] = padded(one["sa_b2"][:, None])
    v["bsa3"] = np.tile(one["sa_b3"], P)[:, None]
    v["bff1"], v["bff2"], v["bffo"] = cols(one["ff_b1"]), cols(one["ff_b2"]), cols(one["out_b"])
    for n, width in PACK:
        assert v[n].shape == (P, width), (n, v[n].shape)
    return np.ascontiguousarray(np.concatenate([v[n] for n, _ in PACK], axis=1))


def kernel(**inputs):
    import concourse.bacc as bacc
    from concourse.bass_utils import run_bass_kernel_spmd

    arrays = {
        "x_dram": np.ascontiguousarray(inputs["x"]).reshape(SAMPLES, C, T),
        "pos_dram": np.ascontiguousarray(inputs["L1_conv_pos_emb"]).reshape(C, T),
        "pack_dram": lay_out(inputs),
    }
    nc = bacc.Bacc("TRN2", target_bir_lowering=False, num_devices=1)
    args = [nc.dram_tensor(n, v.shape, F32, kind="ExternalInput").ap() for n, v in arrays.items()]
    out = nc.dram_tensor("out_dram", (SAMPLES, C, T), F32, kind="ExternalOutput").ap()
    build_program(nc, *args, out, VEC)
    r = run_bass_kernel_spmd(nc, [arrays], core_ids=[0])
    return r.results[0]["out_dram"].reshape(SAMPLES, C, SIDE, SIDE)


VEC = 90
```

```python
from contextlib import ExitStack

import numpy as np

import concourse.bass as bass
from concourse import mybir

F32 = mybir.dt.float32
F32R = mybir.dt.float32r
ALU = mybir.AluOpType
ACT = mybir.ActivationFunctionType
AX = mybir.AxisListType

P = 128
SAMPLES = 8
C = 256
CT = C // P
SIDE = 32
T = SIDE * SIDE
HALF = 512
NH = T // HALF
KT = T // P
D = 32
GROUP = 4
QT = HALF // P

PACK = []
for _l in "0123":
    PACK += [(f"wq{_l}", 512), (f"wk{_l}", 512), (f"wv{_l}", 512)]
    if _l != "1":
        PACK += [(f"wp{_l}", 512)]
PACK += [("mq", 512), ("mk", 512), ("mv", 512), ("ff1", 1024), ("ff2", 512), ("ffo", 512),
         ("sa1", 192), ("sa2", 96), ("sa3", 128), ("ident", P), ("gmean", P)]
for _n in ("0", "pre", "norm", "post", "2", "3"):
    PACK += [(f"gw{_n}", 2), (f"gb{_n}", 2)]
for _l in "023":
    PACK += [(f"bq{_l}", 2), (f"bk{_l}", 2), (f"bv{_l}", 2), (f"bp{_l}", 2)]
PACK += [("bsa1", 1), ("bsa2", 1), ("bsa3", 1), ("bff1", 2), ("bff2", 2), ("bffo", 2)]
AT = {}
_c = 0
for _n, _w in PACK:
    AT[_n] = (_c, _w)
    _c += _w
COLS = _c


class Attention:

    def __init__(self, name, wide, units, ctiles, scale, biased, lead, spread):
        self.name, self.wide, self.units, self.ctiles = name, wide, units, ctiles
        self.scale, self.biased = scale, biased
        self.lead, self.spread = lead, spread
        self.items = 4 if wide else KT
        self.tiles = 1 if wide else 2
        self.slots = self.items // 2 if wide else self.items
        self.maxima = 4 * NH if wide else GROUP * QT * NH
        self.steps = [(u, qh) for u in range(units) for qh in range(NH)]
        self.banks = len(self.steps) * (self.maxima + 1 + wide)
        assert sum(lead) == sum(spread) == self.maxima

    def adder(self, s):
        return "gpsimd" if s + 1 < len(self.steps) else "vector"


NARROW_LEAD, NARROW_SPREAD = [0, 0, 4, 8, 11, 9], [6, 4, 4, 4, 4, 5, 5, 0]
ADDED = 6
P_RING = 3
HEAD_SCALE = 1.0 / float(np.sqrt(D))
ATT0 = Attention("0", False, 2, 1, HEAD_SCALE, True, NARROW_LEAD, NARROW_SPREAD)
ATT1 = Attention("1", False, 2, 1, HEAD_SCALE, False, NARROW_LEAD, NARROW_SPREAD)
ATTM = Attention("m", True, 2, 1, 1.0 / float(np.sqrt(P)), False, [0, 0, 2, 3, 3, 0], [2, 3, 3, 0])
ATT2 = Attention("2", False, 2, 1, HEAD_SCALE, True, NARROW_LEAD, NARROW_SPREAD)
ATT3 = Attention("3", True, 1, 2, 1.0 / float(np.sqrt(C)), True, [0, 0, 0, 0, 8, 0], [2, 3, 3, 0])
LAYERS = (ATT0, ATT1, ATTM, ATT2, ATT3)
NORMS = 6

N_STEPS = sum(len(a.steps) for a in LAYERS)
N_TILES = sum(6 + len(a.steps) * a.items * a.tiles for a in LAYERS) + 2 * NH + 4 + 2 * NH
N_MX = sum(a.banks for a in LAYERS) + 2 * NORMS
N_SLOTS = sum(len(a.steps) * a.slots for a in LAYERS)
assert N_TILES % 2 == 0 and N_MX % 2 == 0
PER = {
    "tile_full": N_TILES, "tile_read0": N_TILES // 2, "tile_read1": N_TILES // 2,
    "mx_full": N_MX, "mx_read": N_MX,
    "p_used": N_SLOTS, "p_summed": sum(len(a.steps) * a.slots if a.wide else ADDED - 1 for a in LAYERS),
    "p_added": sum((ADDED - 1) * (len(a.steps) - 1) for a in LAYERS if not a.wide),
    "added_used": sum(len(a.steps) - 1 for a in LAYERS if not a.wide), "border": 1,
    "acc_ready": sum(len(a.steps) for a in LAYERS if a.wide),
    "av_read": N_STEPS, "av_normed": N_STEPS, "nm_ready": N_STEPS, "row_ready": 16 * N_STEPS,
    "hi_ready": 4 * len(LAYERS),
    "stack_ready0": 16 * 3 * 24, "stack_ready1": 16 * 3 * 24,
    "gn_mean": NORMS, "gn_dev": NORMS, "gn_rstd": NORMS,
    "act_ready": CT * NORMS,
    "x_loaded": 16, "pos_loaded": 16, "x_res_free": 16,
    "vec": 0,
}


class Count:

    def __init__(self, b, before=None):
        self.b, self.n = b, dict(before or {})

    def next(self, name, k=1):
        self.n[name] = self.n.get(name, 0) + k
        return self.at(name, self.n[name])

    def at(self, name, n):
        return self.b * PER[name] + n

    def tile(self):
        self.n["tile"] = self.n.get("tile", -1) + 1
        return self.n["tile"]

    def tile_free(self, n):
        return self.at("tile_read0", 1 + n // 2)

    def tile_read(self, n):
        return self.at("tile_read0", 1 + n // 2 + 1)

    def tile_full(self, n):
        return self.at("tile_full", n + 1)

    def mx(self, k=1):
        self.n["mx"] = self.n.get("mx", -1) + k
        return self.n["mx"]


def build_program(nc, x, pos, pack, out, vec_per_sample):
    PER["vec"] = vec_per_sample
    ctx = ExitStack()
    with ctx:
        def sb(name, shape, dt=F32):
            return ctx.enter_context(nc.sbuf_tensor(name, shape, dt))

        W = sb("weights", [P, COLS])
        ONES = sb("ones", [P, P])
        ONEROW = sb("one_row", [1, P], F32R)
        POWER = sb("power", [P, 2])
        BOUT = sb("folded_bias", [P, 4, CT])
        X = sb("x_res", [P, CT, T])
        A = sb("act_a", [P, CT, T])
        H = sb("act_h", [P, CT, T])
        E = sb("act_e", [P, CT, T])
        AO = sb("att_out", [P, CT, T])
        Q0 = sb("q_hi0", [P, T], F32R)
        K0 = sb("k_hi0", [P, T], F32R)
        VT = sb("v_tokens", [P, KT, C])
        QS = sb("q_stack", [P, NH, 2 * GROUP, HALF], F32R)
        KS = sb("k_stack", [P, 2 * GROUP, T], F32R)
        PR = sb("probs", [P, P_RING, 4, HALF])
        ADD = sb("probs_added", [P, 4, HALF])
        NOTE = sb("note", [P, 2])
        PAUSE = sb("pause", [P, 1])
        MC = sb("max_cols", [P, GROUP * QT, NH])
        NM = sb("neg_max", [P, GROUP * QT])
        NT_ = sb("neg_max_t", [GROUP * QT, P], F32R)
        AVS = sb("av_copy", [P, 2, HALF])
        RC = sb("recip", [P, HALF])
        ST = sb("stats", [P, CT, NH, 6])
        MV = sb("mean_var", [P, CT, 2])
        GM = sb("group_mean", [P, CT])
        DV = sb("deviation", [P, CT])
        SQ = sb("dev_squared", [P, CT])
        VE = sb("var_eps", [P, CT])
        RS = sb("rstd", [P, CT])
        GA = sb("gn_scale", [P, CT])
        GB = sb("gn_shift", [P, CT])

        WT = [ctx.enter_context(nc.psum_tensor(f"work{i}", [P, 2, HALF], F32)) for i in range(2)]
        AVP = ctx.enter_context(nc.psum_tensor("av", [P, HALF], F32))
        AV2 = ctx.enter_context(nc.psum_tensor("av2_or_sums", [P, HALF], F32))
        MX = [ctx.enter_context(nc.psum_tensor(f"mx{i}", [P, HALF], F32)) for i in range(2)]

        ACC = ADD[:, 0, :]
        EDGE = SIDE + 2
        S1 = ADD[0:3 * D, :, :].rearrange("p a b -> p (a b)")[:, 0:EDGE * EDGE].rearrange("p (r c) -> p r c", c=EDGE)
        PRF = PR[:, :, :, :].rearrange("p a b c -> p (a b c)")
        QSF = QS[:, :, :, :].rearrange("p a h n -> p (a h n)")
        S2 = PRF[0:D, 0:T]
        NR = KS[0:1, 0, :].rearrange("o (a n) -> o a n", a=2)

        NARROW_PARTS = {("q", "hi", 0): Q0[:, :], ("k", "hi", 0): K0[:, :]}
        for i, o in enumerate("qk"):
            NARROW_PARTS[o, "lo", 0] = PRF[:, i * T:(i + 1) * T].bitcast(F32R)
            NARROW_PARTS[o, "lo", 1] = PRF[:, (i + 4) * T:(i + 5) * T].bitcast(F32R)
            NARROW_PARTS[o, "hi", 1] = AO[:, i, :].bitcast(F32R)
        WIDE_PARTS = {(o, part, g): QSF[:, (4 * i + 2 * j + g) * T:(4 * i + 2 * j + g + 1) * T]
                      for i, part in enumerate(("hi", "lo")) for j, o in enumerate("qk") for g in range(2)}

        S = {n: ctx.enter_context(nc.semaphore(n)) for n in PER}
        consts = ctx.enter_context(nc.semaphore("consts"))
        folded_mm = ctx.enter_context(nc.semaphore("folded_mm"))
        folded = ctx.enter_context(nc.semaphore("folded"))
        CONSTS = 5

        def w(name, parts=P):
            a, n = AT[name]
            return W[0:parts, a:a + n]

        def wcol(name, i, parts=P, base=0):
            a, _ = AT[name]
            return W[base:base + parts, a + i:a + i + 1]

        def read(slot):
            return S[f"tile_read{slot}"]

        block = ctx.enter_context(nc.Block())

        @block.sync
        def _(sp):
            sp.dma_start(H[:, :, :], x[0].rearrange("(t p) n -> p t n", p=P)).then_inc(S["x_loaded"], 16)
            sp.dma_start(W[:, :], pack).then_inc(S["x_res_free"], 16)
            sp.dma_start(E[:, :, :], pos.rearrange("(t p) n -> p t n", p=P)).then_inc(S["pos_loaded"], 16)
            with sp.Fori(0, SAMPLES) as b:
                c = Count(b)

                def stacks(att):
                    tiles = [c.tile() for _ in range(6)]
                    if att.wide:
                        return
                    for g in range(2):
                        sp.wait_ge(read(tiles[2 * g] % 2), c.tile_read(tiles[2 * g]))
                        sp.wait_ge(read(tiles[2 * g + 1] % 2), c.tile_read(tiles[2 * g + 1]))
                        done = S[f"stack_ready{g}"]
                        for j in range(GROUP):
                            h, rows = GROUP * g + j, slice(D * j, D * j + D)
                            q_hi, q_lo, k_hi, k_lo = (NARROW_PARTS[o, part, g][rows, :].bitcast(F32)
                                                      for o in "qk" for part in ("hi", "lo"))
                            for i, part in enumerate((q_hi, q_lo, q_hi)):
                                sp.dma_start(QS[D * i:D * i + D, :, h, :].bitcast(F32),
                                             part.rearrange("p (a n) -> p a n", a=NH)).then_inc(done, 16)
                            for i, part in enumerate((k_hi, k_hi, k_lo)):
                                sp.dma_start(KS[D * i:D * i + D, h, :].bitcast(F32), part).then_inc(done, 16)

                def skip(att):
                    for _ in range(len(att.steps) * att.items * att.tiles):
                        c.tile()

                stacks(ATT0)
                skip(ATT0)
                for _ in range(NH + 4):
                    c.tile()
                stacks(ATT1)
                skip(ATT1)
                stacks(ATTM)
                skip(ATTM)
                for _ in range(2 * NH):
                    n = c.tile()
                sp.wait_ge(read(n % 2), c.tile_read(n))
                sp.dma_start(H[:, :, :], x[(b + 1) % SAMPLES].rearrange("(t p) n -> p t n", p=P))\
                  .then_inc(S["x_loaded"], 16)
                sp.dma_start(E[:, :, :], pos.rearrange("(t p) n -> p t n", p=P)).then_inc(S["pos_loaded"], 16)
                stacks(ATT2)
                skip(ATT2)
                for _ in range(NH):
                    c.tile()
                stacks(ATT3)
                skip(ATT3)
                sp.wait_ge(S["av_normed"], c.at("av_normed", N_STEPS))
                sp.dma_start(out[b].rearrange("(t p) n -> p t n", p=P), X[:, :, :]).then_inc(S["x_res_free"], 16)
            sp.wait_ge(S["x_res_free"], 16 * (SAMPLES + 1))
            sp.wait_ge(S["x_loaded"], 16 * (SAMPLES + 1))
            sp.wait_ge(S["pos_loaded"], 16 * (SAMPLES + 1))

        @block.gpsimd
        def _(pool):
            pool.memset(ONES[:, :], 1.0).then_inc(consts, 1)
            pool.memset(POWER[:, :], -0.5).then_inc(consts, 1)
            for i, ones in enumerate((ONEROW[:, :], KS[96:97, 0:GROUP, :], KS[96:97, GROUP:, :])):
                pool.wait_ge(consts, 2 + i)
                pool.memset(ones.bitcast(F32), 1.0).then_inc(consts, 1)
            pool.wait_ge(consts, CONSTS)

            def rstd(c):
                n = c.mx(2)
                pool.wait_ge(S["mx_read"], c.at("mx_read", n + 1))
                pool.tensor_tensor(RS[:, :], VE[:, :], POWER[:, :], ALU.pow).then_inc(S["gn_rstd"], 1)

            start = Count(0)
            rstd(start)
            with pool.Fori(0, SAMPLES) as b:
                c = Count(b, start.n)

                def add(att):
                    for _ in range(6):
                        c.tile()
                    c.mx(att.banks)
                    for s in range(len(att.steps)):
                        for i in range(att.items):
                            made = [c.tile() for _ in range(att.tiles)]
                            m = s * att.items + i
                            if att.adder(s) == "gpsimd" and 0 < i < ADDED:
                                for n in made:
                                    pool.wait_ge(read(n % 2), c.tile_read(n))
                                if i == 1:
                                    if steps[0]:
                                        pool.wait_ge(S["added_used"], c.at("added_used", steps[0]))
                                    steps[0] += 1
                                pool.tensor_tensor(ADD[:, :, :], PR[:, (m - 1) % P_RING, :, :] if i == 1 else
                                                   ADD[:, :, :], PR[:, m % P_RING, :, :], ALU.add)\
                                    .then_inc(S["p_added"], 1)
                                pool.wait_ge(S["p_added"], c.next("p_added"))

                steps = [0]
                add(ATT0)
                rstd(c)
                rstd(c)
                for _ in range(NH + 4):
                    c.tile()
                add(ATT1)
                for _ in range(6 + len(ATTM.steps) * ATTM.items * ATTM.tiles + 2 * NH):
                    c.tile()
                c.mx(ATTM.banks)
                rstd(c)
                rstd(c)
                add(ATT2)
                rstd(c)
                c.mx(ATT3.banks - 1)
                rstd(c)

        @block.scalar
        def _(act):
            act.wait_ge(S["x_res_free"], 16)
            act.wait_ge(consts, CONSTS)
            act.wait_ge(folded, 1)
            with act.Fori(0, SAMPLES) as b:
                c = Count(b, {"mx": 1})
                slot = [0]
                slot_end = [0]
                steps = [0]
                summed = [0]

                def row(att, s):
                    u, qh = att.steps[s]
                    if att.wide and s >= 2:
                        c.mx()
                    n = c.mx(att.maxima + 1)
                    act.wait_ge(S["mx_read"], c.at("mx_read", n + 1))
                    dst = NR[0:1, s % 2, :] if att.wide else \
                        QS[96:97, qh, GROUP * u:GROUP * u + GROUP, :].rearrange("o h n -> o (h n)")
                    cols = QT if att.wide else GROUP * QT
                    act.dma_start(dst.rearrange("o (a n) -> o a n", n=P).bitcast(F32),
                                  NT_[0:cols, :].bitcast(F32)).then_inc(S["row_ready"], 16)

                def qkv(att):
                    for i in range(6):
                        if i == 5:
                            row(att, 0)
                        n = c.tile()
                        act.wait_ge(S["tile_full"], c.tile_full(n))
                        src = WT[n % 2][:, :, :].rearrange("p a b -> p (a b)")
                        if i < 4:
                            g, o = i // 2, "qk"[i % 2]
                            dst = (WIDE_PARTS if att.wide else NARROW_PARTS)[o, "hi", g]
                            if att.biased:
                                ins = act.activation(dst, src, ACT.Identity, bias=wcol(f"b{o}{att.name}", g))
                            else:
                                ins = act.activation(dst, src, ACT.Identity)
                            ins.then_inc(S["hi_ready"], 1)
                        else:
                            k = 4 * (i - 4)
                            act.activation(VT[:, k:k + 4, :].rearrange("p a b -> p (a b)"), src, ACT.Identity)\
                               .then_inc(read(n % 2), 1)

                def evacuate(att):
                    act.wait_ge(S["p_used"], c.at("p_used", slot_end[0]))
                    if steps[0]:
                        act.wait_ge(S["av_normed"], c.at("av_normed", steps[0]))
                    ins = act.activation(AVS[:, 0, :], AVP[:, :], ACT.Identity)
                    if not att.wide or att.ctiles == 2:
                        ins = act.activation(AVS[:, 1, :], AV2[:, :], ACT.Identity)
                    ins.then_inc(S["av_read"], 1)
                    steps[0] += 1

                def attention(att):
                    first_slot = slot[0]
                    for s in range(len(att.steps)):
                        for i in range(att.items):
                            if i == att.items - 1 and s + 1 < len(att.steps):
                                row(att, s + 1)
                            for t in range(att.tiles):
                                half = i % 2 if att.wide else t
                                if half == 0 and slot[0] - first_slot >= P_RING:
                                    act.wait_ge(S["p_used"], c.at("p_used", slot[0] - P_RING + 1))
                                    if att.wide:
                                        act.wait_ge(S["p_summed"], c.at("p_summed", summed[0] - P_RING + 1))
                                    else:
                                        before, j = divmod(s * att.items + i - P_RING, att.items)
                                        if j < ADDED and att.adder(before) == "gpsimd":
                                            act.wait_ge(S["p_added"], c.at("p_added", c.n.get("p_added", 0)
                                                                           + (ADDED - 1) * before + max(1, j)))
                                        elif j < ADDED:
                                            act.wait_ge(S["p_summed"], c.at("p_summed", summed[0] + max(1, j)))
                                if half == 0 and not att.wide and s == 0 and i == P_RING - 1:
                                    act.wait_ge(S["stack_ready1"], c.next("stack_ready1", 16 * 24))
                                n = c.tile()
                                act.wait_ge(S["tile_full"], c.tile_full(n))
                                buffer = PR[:, (slot[0] - first_slot) % P_RING, :, :]
                                act.activation(buffer[:, 2 * half:2 * half + 2, :], WT[n % 2][:, :, :], ACT.Exp,
                                               scale=att.scale).then_inc(read(n % 2), 1)
                                if half == 1:
                                    slot[0] += 1
                                    if att.wide:
                                        summed[0] += 1
                            if i == 0 and s > 0:
                                evacuate(att)
                        slot_end[0] = slot[0]
                    if att.wide:
                        c.mx(2)
                    else:
                        summed[0] += ADDED - 1
                        c.next("p_added", (ADDED - 1) * (len(att.steps) - 1))
                    evacuate(att)

                for att in LAYERS:
                    c.mx({ATT1: 4, ATT2: 4, ATT3: 2}.get(att, 0))
                    qkv(att)
                    attention(att)
                    if att in (ATT0, ATT2):
                        for _ in range(NH):
                            c.tile()
                    if att is ATT0:
                        act.wait_ge(S["border"], c.next("border"))
                        n = c.tile()
                        act.wait_ge(S["tile_full"], c.tile_full(n))
                        for j in range(3):
                            ins = act.activation(
                                S1[D * j:D * j + D, 1:SIDE + 1, 2 - j:2 - j + SIDE],
                                WT[n % 2][D * j:D * j + D, :, :].rearrange("p a (r c) -> p (a r) c", c=SIDE),
                                ACT.Silu, bias=wcol("bsa1", 0, D, D * j))
                        ins.then_inc(read(n % 2), 1)
                        n = c.tile()
                        act.wait_ge(S["tile_full"], c.tile_full(n))
                        act.activation(S2[:, :], WT[n % 2][0:D, :, :].rearrange("p a b -> p (a b)"), ACT.Silu,
                                       bias=wcol("bsa2", 0, D)).then_inc(read(n % 2), 1)
                        for nh in range(NH):
                            n = c.tile()
                            act.wait_ge(S["tile_full"], c.tile_full(n))
                            act.activation(AO[:, 0, nh * HALF:(nh + 1) * HALF], WT[n % 2][:, 0, :], ACT.Sigmoid,
                                           bias=wcol("bsa3", 0)).then_inc(read(n % 2), 1)
                    if att is ATTM:
                        for dst, bias, func in ((H, w("bff1"), ACT.Silu), (A, BOUT[:, 3, :], ACT.Identity)):
                            for nh in range(NH):
                                n = c.tile()
                                act.wait_ge(S["tile_full"], c.tile_full(n))
                                for m in range(CT):
                                    ins = act.activation(dst[:, m, nh * HALF:(nh + 1) * HALF], WT[n % 2][:, m, :],
                                                         func, bias=bias[:, m:m + 1])
                                ins.then_inc(read(n % 2), 1)

        @block.vector
        def _(dve):
            dve.wait_ge(S["x_res_free"], 16)
            total = {}

            def chain(c, ins):
                ins.then_inc(S["vec"], 1)
                dve.wait_ge(S["vec"], c.next("vec"))

            def stats(src, nh):
                for t in range(CT):
                    ins = dve.bn_stats(ST[:, t, nh, :], src[:, t, nh * HALF:(nh + 1) * HALF])
                return ins

            def norm_means(c, last_stats):
                chain(c, last_stats)
                dve.memset(PAUSE[:, :], 0.0)
                for t in range(CT):
                    ins = dve.bn_aggr(MV[:, t, :], ST[:, t, :, :].rearrange("p a b -> p (a b)"))
                ins.then_inc(S["gn_mean"], 1)
                dve.wait_ge(S["gn_mean"], c.next("gn_mean"))

            def norm_deviations(c):
                n = c.mx()
                dve.wait_ge(S["mx_full"], c.at("mx_full", n + 1))
                chain(c, dve.tensor_tensor(DV[:, :], MV[:, :, 0], MX[n % 2][:, 0:CT], ALU.subtract))
                dve.tensor_tensor(SQ[:, :], DV[:, :], DV[:, :], ALU.mult).then_inc(S["gn_dev"], 1)
                dve.tensor_copy(GM[:, :], MX[n % 2][:, 0:CT]).then_inc(S["mx_read"], 1)

            def norm_variances(c, eps):
                n = c.mx()
                dve.wait_ge(S["mx_full"], c.at("mx_full", n + 1))
                dve.tensor_scalar(VE[:, :], MX[n % 2][:, 0:CT], eps, None, ALU.add).then_inc(S["mx_read"], 1)

            def norm_scales(c, name):
                dve.wait_ge(S["gn_rstd"], c.next("gn_rstd"))
                chain(c, dve.tensor_tensor(GA[:, :], RS[:, :], w(f"gw{name}"), ALU.mult))
                for t in range(CT):
                    ins = dve.scalar_tensor_tensor(out=GB[:, t:t + 1], in0=GM[:, t:t + 1], scalar=GA[:, t:t + 1],
                                                   in1=wcol(f"gb{name}", t), op0=ALU.mult, op1=ALU.subtract)
                chain(c, ins)

            def norm_apply(src, dst, t):
                return dve.tensor_scalar(dst[:, t, :], src[:, t, :], GA[:, t:t + 1], GB[:, t:t + 1], ALU.mult,
                                         ALU.subtract)

            def norm(c, src, name, eps, given=False):
                for nh in range(NH):
                    if not (given and nh + 1 < NH):
                        ins = stats(src, nh)
                norm_means(c, ins)
                norm_deviations(c)
                norm_variances(c, eps)
                norm_scales(c, name)

            def apply_to(c, src, dst):
                for t in range(CT):
                    norm_apply(src, dst, t).then_inc(S["act_ready"], 1)
                    c.next("act_ready")

            start = Count(0)
            dve.wait_ge(S["x_loaded"], start.next("x_loaded", 16))
            norm(start, H, "0", 1e-5)
            apply_to(start, H, A)
            dve.wait_ge(folded_mm, 1)
            for i, name in enumerate(("bp0", "bp2", "bp3", "bffo")):
                ins = dve.tensor_tensor(BOUT[:, i, :], WT[1][:, 0, C + CT * i:C + CT * i + CT], w(name), ALU.add)
            ins.then_inc(folded, 1)
            for i, name in enumerate(("ff2", "wv3")):
                dve.tensor_copy(w(name).rearrange("p (k n) -> p k n", n=C), WT[i][:, :, 0:C]).then_inc(read(i), 1)
            with dve.Fori(0, SAMPLES) as b:
                c = Count(b, start.n)

                def maxima(att, k):
                    for _ in range(k):
                        n = c.mx()
                        i = mi[0]
                        mi[0] += 1
                        dve.wait_ge(S["mx_full"], c.at("mx_full", n + 1))
                        if att.wide:
                            col, kh = i // NH, i % NH
                        else:
                            qt, kh, j = i // (NH * GROUP), i // GROUP % NH, i % GROUP
                            col = j * QT + qt
                        dve.tensor_reduce(MC[:, col, kh:kh + 1], MX[n % 2][:, :], AX.X, ALU.max)\
                           .then_inc(S["mx_read"], 1)
                    if mi[0] == att.maxima and k:
                        cols = QT if att.wide else GROUP * QT
                        dve.wait_ge(S["mx_read"], c.at("mx_read", n + 1))
                        dve.tensor_reduce(NM[:, 0:cols], MC[:, 0:cols, :], AX.X, ALU.max, negate=True)\
                           .then_inc(S["nm_ready"], 1)
                        c.next("nm_ready")

                mi = [0]

                def columns(att):
                    cols = QT if att.wide else GROUP * QT
                    n = c.mx()
                    if c.n.get("row_ready"):
                        dve.wait_ge(S["row_ready"], c.at("row_ready", c.n["row_ready"]))
                    dve.wait_ge(S["mx_full"], c.at("mx_full", n + 1))
                    dve.tensor_copy(NT_[0:cols, :], MX[n % 2][0:cols, 0:P]).then_inc(S["mx_read"], 1)
                    c.next("row_ready", 16)
                    mi[0] = 0

                def qkv(att):
                    parts = WIDE_PARTS if att.wide else NARROW_PARTS
                    for i in range(6):
                        n = c.tile()
                        maxima(att, att.lead[i])
                        if i < 4:
                            g, o = i // 2, "qk"[i % 2]
                            dve.wait_ge(S["hi_ready"], c.next("hi_ready"))
                            dve.scalar_tensor_tensor(
                                out=parts[o, "lo", g], in0=WT[n % 2][:, :, :].rearrange("p a b -> p (a b)"),
                                scalar=wcol(f"b{o}{att.name}", g) if att.biased else 0.0,
                                in1=parts[o, "hi", g].bitcast(F32), op0=ALU.add, op1=ALU.subtract)\
                                .then_inc(read(n % 2), 1)
                    columns(att)

                def take_sums():
                    n = c.mx()
                    dve.wait_ge(S["mx_full"], c.at("mx_full", n + 1))
                    dve.tensor_copy(RC[:, :], MX[n % 2][:, :]).then_inc(S["mx_read"], 1)
                    dve.wait_ge(S["mx_read"], c.at("mx_read", n + 1))

                def normalize(att, s, dst, taken=False):
                    u, qh = att.steps[s]
                    cols = slice(qh * HALF, (qh + 1) * HALF)
                    if taken:
                        chain(c, dve.reciprocal(RC[:, :], RC[:, :]))
                        dve.wait_ge(S["av_read"], c.next("av_read"))
                    elif att.wide:
                        n = c.mx()
                        dve.wait_ge(S["mx_full"], c.at("mx_full", n + 1))
                        dve.reciprocal(RC[:, :], MX[n % 2][:, :]).then_inc(S["mx_read"], 1)
                        dve.wait_ge(S["mx_read"], c.at("mx_read", n + 1))
                        dve.wait_ge(S["av_read"], c.next("av_read"))
                    else:
                        dve.wait_ge(S["av_read"], c.next("av_read"))
                        chain(c, dve.reciprocal(RC[:, :], AVS[:, 1, :]))
                    for d in range(att.ctiles):
                        ins = dve.tensor_tensor(dst[:, u + d, cols], AVS[:, d, :], RC[:, :], ALU.mult)
                    if att is ATT3:
                        chain(c, ins)
                        for d in range(CT):
                            ins = dve.scalar_tensor_tensor(out=X[:, d, cols], in0=AO[:, d, cols],
                                                           scalar=BOUT[:, 2, d:d + 1], in1=X[:, d, cols],
                                                           op0=ALU.add, op1=ALU.add)
                    ins.then_inc(S["av_normed"], 1)

                def accumulate(att, i):
                    n = c.tile()
                    dve.wait_ge(read(n % 2), c.tile_read(n))
                    half, m = i % 2, wide_slot[0]
                    for jj in range(2):
                        pt = PR[:, m % P_RING, 2 * half + jj, :]
                        if i == 0 and jj == 0:
                            continue
                        prev = PR[:, m % P_RING, 0, :] if i == 0 else ACC
                        ins = dve.tensor_tensor(ACC, prev, pt, ALU.add)
                        if i == att.items - 1 and jj == 1:
                            chain(c, ins)
                            dve.tensor_copy(NOTE[:, 0:1], ADD[:, 0, 0:1]).then_inc(S["acc_ready"], 1)
                            dve.tensor_copy(NOTE[:, 1:2], ADD[:, 0, 0:1]).then_inc(S["p_summed"], 1)
                        elif half == 1 and jj == 1:
                            ins.then_inc(S["p_summed"], 1)
                            dve.wait_ge(S["p_summed"], c.at("p_summed", c.n.get("p_summed", 0) + 1))
                        else:
                            chain(c, ins)
                    if half == 1:
                        c.next("p_summed")
                        wide_slot[0] += 1

                wide_slot = [0]

                def attention(att, dst):
                    wide_slot[0] = 0
                    steps = len(att.steps)
                    for s in range(steps):
                        for i in range(att.items):
                            if s + 1 < steps:
                                maxima(att, att.spread[i])
                                if i == att.items - 1:
                                    columns(att)
                            if s > 0 and att.wide and i == 0:
                                if s + 1 < steps:
                                    take_sums()
                                else:
                                    normalize(att, s - 1, dst)
                            elif s > 0 and i == att.items - 1 and not (att.wide and s + 1 == steps):
                                normalize(att, s - 1, dst, taken=att.wide)
                            if att.wide:
                                accumulate(att, i)
                            else:
                                made = [c.tile() for _ in range(att.tiles)]
                                if att.adder(s) == "vector" and 0 < i < ADDED:
                                    for n in made:
                                        dve.wait_ge(read(n % 2), c.tile_read(n))
                                    m = s * att.items + i
                                    dve.tensor_tensor(ADD[:, :, :], PR[:, (m - 1) % P_RING, :, :] if i == 1 else
                                                      ADD[:, :, :], PR[:, m % P_RING, :, :], ALU.add)\
                                       .then_inc(S["p_summed"], 1)
                                    dve.wait_ge(S["p_summed"], c.next("p_summed"))
                            if att is ATT3 and s + 1 == steps:
                                if i == 0:
                                    dve.wait_ge(S["x_loaded"], c.next("x_loaded", 16))
                                    stats(H, 0)
                                    norm_means(c, stats(H, 1))
                                elif i == 1:
                                    norm_deviations(c)
                                elif i == 2:
                                    norm_variances(c, 1e-5)
                                else:
                                    norm_scales(c, "0")
                                    apply_to(c, H, A)
                    normalize(att, steps - 1, dst)

                def project(i, residual):
                    for nh in range(NH):
                        n = c.tile()
                        dve.wait_ge(S["tile_full"], c.tile_full(n))
                        for m in range(CT):
                            cols = slice(nh * HALF, (nh + 1) * HALF)
                            ins = dve.scalar_tensor_tensor(out=X[:, m, cols], in0=WT[n % 2][:, m, :],
                                                           scalar=BOUT[:, i, m:m + 1], in1=residual[:, m, cols],
                                                           op0=ALU.add, op1=ALU.add)
                        ins.then_inc(read(n % 2), 1)
                        dve.wait_ge(read(n % 2), c.tile_read(n))
                        if nh == 0:
                            stats(X, 0)

                qkv(ATT0)
                attention(ATT0, AO)
                dve.memset(S1, 0.0).then_inc(S["border"], 1)
                dve.wait_ge(S["x_res_free"], c.next("x_res_free", 16))
                project(0, H)

                norm(c, X, "pre", 1e-6, given=True)
                dve.wait_ge(S["pos_loaded"], c.next("pos_loaded", 16))
                for t in range(CT):
                    ins = norm_apply(X, A, t)
                chain(c, ins)
                for t in range(CT):
                    dve.tensor_tensor(A[:, t, :], A[:, t, :], E[:, t, :], ALU.add).then_inc(S["act_ready"], 1)
                dve.wait_ge(S["act_ready"], c.next("act_ready", CT))
                norm(c, A, "norm", 1e-6)
                apply_to(c, A, H)
                for _ in range(2):
                    c.tile()
                for nh in range(NH):
                    n = c.tile()
                    dve.wait_ge(read(n % 2), c.tile_read(n))
                for t in range(CT):
                    dve.tensor_tensor(E[:, t, :], A[:, t, :], AO[:, 0, :], ALU.mult).then_inc(S["act_ready"], 1)
                    c.next("act_ready")
                dve.wait_ge(S["act_ready"], c.at("act_ready", c.n["act_ready"]))
                qkv(ATT1)
                attention(ATT1, AO)
                qkv(ATTM)
                attention(ATTM, A)
                for _ in range(NH):
                    c.tile()
                for nh in range(NH):
                    n = c.tile()
                    dve.wait_ge(read(n % 2), c.tile_read(n))
                    if nh == 0:
                        stats(A, 0)
                norm(c, A, "post", 1e-6, given=True)
                for t in range(CT):
                    ins = dve.scalar_tensor_tensor(out=X[:, t, :], in0=A[:, t, :], scalar=GA[:, t:t + 1],
                                                   in1=X[:, t, :], op0=ALU.mult, op1=ALU.add)
                chain(c, ins)
                for t in range(CT):
                    ins = dve.tensor_scalar(X[:, t, :], X[:, t, :], GB[:, t:t + 1], None, ALU.subtract)
                chain(c, ins)

                norm(c, X, "2", 1e-5)
                apply_to(c, X, A)
                qkv(ATT2)
                attention(ATT2, AO)
                project(1, A)

                norm(c, X, "3", 1e-5, given=True)
                apply_to(c, X, A)
                qkv(ATT3)
                attention(ATT3, AO)
                total.update(c.n)
            assert total["vec"] - start.n["vec"] == PER["vec"], f"vec {total['vec'] - start.n['vec']}"
            assert total["act_ready"] - start.n["act_ready"] == PER["act_ready"], total
            assert total["tile"] + 1 == N_TILES and total["mx"] - start.n["mx"] == N_MX, (total, N_TILES, N_MX)

        @block.tensor
        def _(pe):
            def mm(dst, lhsT, rhs, start, stop, **kw):
                return nc.tensor.matmul(dst, lhsT, rhs, start=start, stop=stop, **kw)

            pe.wait_ge(S["x_res_free"], 16)
            pe.wait_ge(consts, CONSTS)
            total = {}

            def new_bank(c):
                n = c.mx()
                if n >= 2:
                    pe.wait_ge(S["mx_read"], c.at("mx_read", n - 1))
                return MX[n % 2]

            def group_means(c):
                bank = new_bank(c)
                pe.wait_ge(S["gn_mean"], c.next("gn_mean"))
                mm(bank[:, 0:CT], w("gmean"), MV[:, :, 0], True, True).then_inc(S["mx_full"], 1)

            def group_variances(c):
                bank = new_bank(c)
                mm(bank[:, 0:CT], w("gmean"), MV[:, :, 1], True, False)
                pe.wait_ge(S["gn_dev"], c.next("gn_dev"))
                mm(bank[:, 0:CT], w("gmean"), SQ[:, :], False, True).then_inc(S["mx_full"], 1)

            def groups(c):
                group_means(c)
                group_variances(c)

            start = Count(0)
            groups(start)
            start.next("act_ready", 2)
            for i, (first, second) in enumerate((("ff2", "ffo"), ("wv3", "wp3"))):
                first, second = (w(name).rearrange("p (k n) -> p k n", n=C) for name in (first, second))
                for m in range(CT):
                    for k in range(CT):
                        mm(WT[i][:, m, 0:C], first[:, k, m * P:(m + 1) * P], second[:, k, :], k == 0, k == CT - 1)
            for i, (name, bias) in enumerate((("wp0", "bv0"), ("wp2", "bv2"), ("wp3", "bv3"), ("ffo", "bff2"))):
                wp = w(name).rearrange("p (k n) -> p k n", n=C)
                for m in range(CT):
                    for k in range(CT):
                        ins = mm(WT[1][:, 0, C + CT * i + m:C + CT * i + m + 1], wp[:, k, m * P:(m + 1) * P],
                                 wcol(bias, k), k == 0, k == CT - 1)
            ins.then_inc(folded_mm, 1)
            with pe.Fori(0, SAMPLES) as b:
                c = Count(b, start.n)

                def new_tile():
                    n = c.tile()
                    pe.wait_ge(read(n % 2), c.tile_free(n))
                    return n, WT[n % 2]

                mi = [0]
                stacked = [False]

                def maxima(att, s, k):
                    for _ in range(k):
                        u, qh = att.steps[s]
                        i = mi[0]
                        mi[0] += 1
                        bank = new_bank(c)
                        if att.wide:
                            qt, kh = i // NH, i % NH
                            q0 = qh * HALF + qt * P
                            for ct in range(att.ctiles):
                                ins = mm(bank[:, :], WIDE_PARTS["q", "hi", u + ct][:, q0:q0 + P],
                                         WIDE_PARTS["k", "hi", u + ct][:, kh * HALF:(kh + 1) * HALF],
                                         ct == 0, ct == att.ctiles - 1)
                        else:
                            qt, kh, j = i // (NH * GROUP), i // GROUP % NH, i % GROUP
                            q0 = qh * HALF + qt * P
                            if s == 0 and not stacked[0]:
                                r = slice(D * j, D * j + D)
                                ins = mm(bank[:, :], Q0[r, q0:q0 + P], K0[r, kh * HALF:(kh + 1) * HALF], True, True,
                                         tile_position=(D * j, 0))
                            else:
                                h = GROUP * u + j
                                ins = mm(bank[:, :], QS[0:96, qh, h, qt * P:(qt + 1) * P],
                                         KS[0:96, h, kh * HALF:(kh + 1) * HALF], True, True)
                        ins.then_inc(S["mx_full"], 1)

                def columns(att):
                    cols = QT if att.wide else GROUP * QT
                    bank = new_bank(c)
                    pe.wait_ge(S["nm_ready"], c.next("nm_ready"))
                    nc.tensor.transpose(bank[0:cols, 0:P], NM[:, 0:cols], w("ident")).then_inc(S["mx_full"], 1)
                    mi[0] = 0

                def input_ready(k):
                    pe.wait_ge(S["act_ready"], c.next("act_ready"))

                def qkv(att, src_q, src_kv, wq, wk, wv, ready=input_ready):
                    tiles = []
                    stacked[0] = False
                    for i in range(6):
                        n, tile = new_tile()
                        tiles.append(n)
                        done = [0]
                        if i == 5 and not att.wide:
                            pe.wait_ge(S["stack_ready0"], c.next("stack_ready0", 16 * 24))
                            stacked[0] = True

                        def between(part):
                            k = int(part * att.lead[i]) - done[0]
                            done[0] += k
                            if k and mi[0] == 0:
                                for t in tiles[2:4] if att.ctiles == 2 else tiles[:2]:
                                    pe.wait_ge(read(t % 2), c.tile_read(t))
                            maxima(att, 0, k)

                        if i < 4:
                            g, src, wt = i // 2, (src_q, src_kv)[i % 2], w((wq, wk)[i % 2])
                            wt = wt.rearrange("p (g k n) -> p g k n", g=2, k=CT)
                            for k in range(CT):
                                if i == 0:
                                    ready(k)
                                for nh in range(NH):
                                    between((2 * k + nh) / 4 if i > 2 or k else 0)
                                    ins = mm(tile[:, nh, :], wt[:, g, k, :], src[:, k, nh * HALF:(nh + 1) * HALF],
                                             k == 0, k == CT - 1)
                        else:
                            wt = w(wv).rearrange("p (k n) -> p k n", k=CT)
                            for t in range(4):
                                tok = (4 * (i - 4) + t) * P
                                for k in range(CT):
                                    between(min(1, (2 * t + k) / (8 if i < 5 else 3)))
                                    if i == 5 and t == 1 and k == 1:
                                        columns(att)
                                    ins = mm(tile[:, t // 2, t % 2 * C:(t % 2 + 1) * C], src_kv[:, k, tok:tok + P],
                                             wt[:, k, :], k == 0, k == CT - 1)
                        ins.then_inc(S["tile_full"], 1)
                        between(1)

                def scores(att, s, i, between):
                    u, qh = att.steps[s]
                    qs = slice(qh * HALF, (qh + 1) * HALF)
                    made = []
                    for t in range(att.tiles):
                        n, tile = new_tile()
                        made.append(n)
                        for jj in range(2):
                            if att.wide:
                                ks = slice((2 * i + jj) * P, (2 * i + jj + 1) * P)
                                for ct in range(att.ctiles):
                                    k_hi, k_lo, q_hi, q_lo = (WIDE_PARTS[o, part, u + ct][:, x] for o, x in
                                                              (("k", ks), ("q", qs)) for part in ("hi", "lo"))
                                    mm(tile[:, jj, :], k_hi, q_hi, ct == 0, False)
                                    mm(tile[:, jj, :], k_hi, q_lo, False, False)
                                    mm(tile[:, jj, :], k_lo, q_hi, False, False)
                                ins = mm(tile[:, jj, :], ONEROW[:, :], NR[0:1, s % 2, :], False, True)
                                if jj == 0:
                                    between()
                            else:
                                h = GROUP * u + 2 * t + jj
                                ins = mm(tile[:, jj, :], KS[0:97, h, i * P:(i + 1) * P], QS[0:97, qh, h, :],
                                         True, True)
                        ins.then_inc(S["tile_full"], 1)
                        between()
                    return made

                slot = [0]
                step = [0]

                def values(att, s, i, made, between):
                    u, _ = att.steps[s]
                    for n in made:
                        pe.wait_ge(read(n % 2), c.tile_read(n))
                    if i == 0:
                        if step[0]:
                            pe.wait_ge(S["av_read"], c.at("av_read", step[0]))
                        step[0] += 1
                    pt = PR[:, slot[0] % P_RING, :, :]
                    if att.wide:
                        for jj in range(2):
                            kt = 2 * i + jj
                            for d in range(att.ctiles):
                                col = (u + d) * P
                                ins = mm((AVP, AV2)[d][:, :], VT[:, kt, col:col + P], pt[:, 2 * (i % 2) + jj, :],
                                         kt == 0, kt == KT - 1)
                            if jj == 1 and i % 2 == 1:
                                ins.then_inc(S["p_used"], 1)
                                c.next("p_summed")
                                slot[0] += 1
                            between()
                        if i == att.items - 1:
                            bank = new_bank(c)
                            pe.wait_ge(S["acc_ready"], c.next("acc_ready"))
                            mm(bank[:, :], ONES[:, :], ACC, True, True).then_inc(S["mx_full"], 1)
                        return

                    def sums(p, start, stop):
                        for j in range(GROUP):
                            ins = mm(AV2[D * j:D * j + D, :], ONES[:, 0:D], p[:, j, :], start, stop,
                                     tile_position=(0, D * j))
                        return ins

                    for j in range(GROUP):
                        h = GROUP * u + j
                        ins = mm(AVP[D * j:D * j + D, :], VT[:, i, D * h:D * h + D], pt[:, j, :], i == 0,
                                 i == KT - 1, tile_position=(0, D * j))
                    if i < ADDED:
                        ins.then_inc(S["p_used"], 1)
                    between()
                    between()
                    if i >= ADDED:
                        if i == KT - 1:
                            if att.adder(s) == "gpsimd":
                                pe.wait_ge(S["p_added"], c.next("p_added", ADDED - 1))
                                sums(ADD, False, False).then_inc(S["added_used"], 1)
                            else:
                                pe.wait_ge(S["p_summed"], c.next("p_summed", ADDED - 1))
                                sums(ADD, False, False)
                            between()
                        sums(pt, i == ADDED, i == KT - 1).then_inc(S["p_used"], 1)
                        between()
                    slot[0] += 1

                def attention(att):
                    behind = None
                    slot[0] = 0
                    for s in range(len(att.steps)):
                        for i in range(att.items):
                            more = s + 1 < len(att.steps)
                            if i == 0:
                                pe.wait_ge(S["row_ready"], c.next("row_ready", 16))
                                if s == 1 and not att.wide:
                                    pe.wait_ge(S["stack_ready1"], c.next("stack_ready1", 16 * 24))
                            left = [att.spread[i] if more else 0]

                            def between():
                                if left[0]:
                                    left[0] -= 1
                                    maxima(att, s + 1, 1)

                            if more and i == att.items - 1 and att.wide:
                                columns(att)
                            made = scores(att, s, i, between)
                            if more and i == att.items - 1 and not att.wide:
                                columns(att)
                            if behind is not None:
                                if att.wide and i == 0:
                                    maxima(att, s + 1, left[0])
                                    left[0] = 0
                                values(att, *behind, between)
                            if left[0]:
                                maxima(att, s + 1, left[0])
                            if att is ATT3 and s == 1:
                                if i == 1:
                                    group_means(c)
                                elif i == 2:
                                    group_variances(c)
                            behind = (s, i, made)
                    values(att, *behind, lambda: None)

                def dense(srcs, weights, ready):
                    wt = w(weights).rearrange("p (k n) -> p k n", n=C)
                    made = []
                    for nh in range(NH):
                        n, tile = new_tile()
                        ready(nh)
                        made.append(n)
                        for m in range(CT):
                            for k in range(CT * len(srcs)):
                                ins = mm(tile[:, m, :], wt[:, k, m * P:(m + 1) * P],
                                         srcs[k // CT][:, k % CT, nh * HALF:(nh + 1) * HALF],
                                         k == 0, k == CT * len(srcs) - 1)
                        ins.then_inc(S["tile_full"], 1)
                    return made

                def normed(nh):
                    pe.wait_ge(S["av_normed"], c.at("av_normed", step[0] - 1 + nh))

                def wait_tiles(made):
                    def ready(nh):
                        pe.wait_ge(read(made[nh] % 2), c.tile_read(made[nh]))
                    return ready

                qkv(ATT0, A, A, "wq0", "wk0", "wv0",
                    lambda k: pe.wait_ge(S["act_ready"], c.at("act_ready", c.n["act_ready"] - 1 + k)))
                attention(ATT0)
                dense([AO], "wp0", normed)

                groups(c)
                n, tile = new_tile()
                w1 = w("sa1").rearrange("p (k n) -> p k n", k=CT)
                for k in range(CT):
                    input_ready(k)
                    for nh in range(NH):
                        ins = mm(tile[0:3 * D, nh, :], w1[:, k, :], A[:, k, nh * HALF:(nh + 1) * HALF],
                                 k == 0, k == CT - 1)
                ins.then_inc(S["tile_full"], 1)
                groups(c)
                pe.wait_ge(read(n % 2), c.tile_read(n))
                n, tile = new_tile()
                w2 = w("sa2", 3 * D).rearrange("p (k n) -> p k n", k=3)
                rows = SIDE // NH
                for nh in range(NH):
                    for dy in range(3):
                        ins = mm(tile[0:D, nh, :], w2[:, dy, :],
                                 S1[:, dy + rows * nh:dy + rows * (nh + 1), 1:SIDE + 1], dy == 0, dy == 2)
                ins.then_inc(S["tile_full"], 1)
                pe.wait_ge(read(n % 2), c.tile_read(n))
                for nh in range(NH):
                    n, tile = new_tile()
                    mm(tile[:, 0, :], w("sa3", D), S2[:, nh * HALF:(nh + 1) * HALF], True, True)\
                        .then_inc(S["tile_full"], 1)
                qkv(ATT1, H, H, "wq1", "wk1", "wv1")
                attention(ATT1)
                qkv(ATTM, E, H, "mq", "mk", "mv")
                attention(ATTM)
                made = dense([AO, A], "ff1", normed)
                dense([H], "ff2", wait_tiles(made))
                groups(c)

                groups(c)
                qkv(ATT2, A, A, "wq2", "wk2", "wv2")
                attention(ATT2)
                dense([AO], "wp2", normed)

                groups(c)
                qkv(ATT3, A, A, "wq3", "wk3", "wv3")
                attention(ATT3)
                c.next("act_ready", 2)
                total.update(c.n)
            assert total["tile"] + 1 == N_TILES and total["mx"] - start.n["mx"] == N_MX, (total, N_TILES, N_MX)


def lay_out(a):
    f = np.float32

    def rows(m, order):
        return np.asarray(m)[order]

    def stationary(m):
        return np.asarray(m).reshape(2, P, CT, P).transpose(3, 0, 2, 1).reshape(P, -1)

    def moving(m):
        m = np.asarray(m)
        return m.reshape(m.shape[0], -1, P).transpose(2, 1, 0).reshape(P, -1)

    def plain_rows(m):
        m = np.asarray(m)
        return m.reshape(CT, P, C).transpose(1, 0, 2).reshape(P, -1)

    def cols(v):
        return np.asarray(v).reshape(CT, P).T

    def padded(m):
        m = np.asarray(m)
        return np.concatenate([m, np.zeros((P - m.shape[0], m.shape[1]), f)])

    heads = np.arange(3 * C).reshape(C // D, 3, D)
    split = [heads[:, i].reshape(-1) for i in range(3)]
    plain = [np.arange(C) + i * C for i in range(3)]
    v = {}
    for l, order, proj in (("0", split, "proj"), ("2", split, "proj"), ("3", plain, "out")):
        wt, bs = a[f"L{l}_conv_qkv_w"], a[f"L{l}_conv_qkv_b"]
        v[f"wq{l}"], v[f"wk{l}"] = (stationary(rows(wt, order[i])) for i in range(2))
        v[f"wv{l}"] = moving(rows(wt, order[2]))
        v[f"wp{l}"] = moving(a[f"L{l}_conv_{proj}_w"])
        for i, n in enumerate(("bq", "bk", "bv")):
            v[f"{n}{l}"] = cols(rows(bs, order[i]))
        v[f"bp{l}"] = cols(a[f"L{l}_conv_{proj}_b"])
        v[f"gw{l}"], v[f"gb{l}"] = cols(a[f"L{l}_conv_gn_w"]), cols(a[f"L{l}_conv_gn_b"])
    one = {k[8:]: np.asarray(x) for k, x in a.items() if k.startswith("L1_conv_")}
    v["wq1"], v["wk1"], v["wv1"] = stationary(one["wq"]), stationary(one["wk"]), moving(one["wv"])
    v["mq"] = stationary(np.concatenate([one["wq0"], one["wq1"]]))
    v["mk"] = stationary(np.concatenate([one["wk0"], one["wk1"]]))
    v["mv"] = moving(np.concatenate([one["wv0"], one["wv1"]]))
    v["ff1"], v["ff2"], v["ffo"] = moving(one["ff_w1"]), plain_rows(one["ff_w2"]), moving(one["out_w"])
    v["wv3"] = plain_rows(a["L3_conv_qkv_w"][2 * C:])
    v["sa1"] = moving(np.tile(one["sa_w1"].reshape(D, C), (3, 1)))
    v["sa2"] = padded(one["sa_w2"].transpose(3, 1, 2, 0).reshape(3 * D, 3 * D))
    v["sa3"] = padded(np.tile(one["sa_w3"].reshape(1, D), (P, 1)).T)
    v["ident"] = np.eye(P, dtype=f)
    v["gmean"] = np.kron(np.eye(P // 8, dtype=f), np.full((8, 8), 1 / 8, f))
    for n in ("pre", "norm", "post"):
        v[f"gw{n}"], v[f"gb{n}"] = cols(one[f"{n}_g"]), cols(one[f"{n}_b"])
    v["bsa1"] = padded(np.tile(one["sa_b1"], 3)[:, None])
    v["bsa2"] = padded(one["sa_b2"][:, None])
    v["bsa3"] = np.tile(one["sa_b3"], P)[:, None]
    v["bff1"], v["bff2"], v["bffo"] = cols(one["ff_b1"]), cols(one["ff_b2"]), cols(one["out_b"])
    for n, width in PACK:
        assert v[n].shape == (P, width), (n, v[n].shape)
    return np.ascontiguousarray(np.concatenate([v[n] for n, _ in PACK], axis=1))


def kernel(**inputs):
    import concourse.bacc as bacc
    from concourse.bass_utils import run_bass_kernel_spmd

    arrays = {
        "x_dram": np.ascontiguousarray(inputs["x"]).reshape(SAMPLES, C, T),
        "pos_dram": np.ascontiguousarray(inputs["L1_conv_pos_emb"]).reshape(C, T),
        "pack_dram": lay_out(inputs),
    }
    nc = bacc.Bacc("TRN2", target_bir_lowering=False, num_devices=1)
    args = [nc.dram_tensor(n, v.shape, F32, kind="ExternalInput").ap() for n, v in arrays.items()]
    out = nc.dram_tensor("out_dram", (SAMPLES, C, T), F32, kind="ExternalOutput").ap()
    build_program(nc, *args, out, VEC)
    r = run_bass_kernel_spmd(nc, [arrays], core_ids=[0])
    return r.results[0]["out_dram"].reshape(SAMPLES, C, SIDE, SIDE)


VEC = 79
```
